# Optimizing a Trainium2 kernel written in Bass

```python
import numpy as np
import jax
import jax.numpy as jnp

def _softmax(x, axis=-1):
    return jax.nn.softmax(x, axis=axis)

def _gelu(x):
    return jax.nn.gelu(x, approximate=True)

def _silu(x):
    return jax.nn.silu(x)

def _sigmoid(x):
    return jax.nn.sigmoid(x)

def _layernorm(x, axis=-1, eps=1e-05):
    m = jnp.mean(x, axis=axis, keepdims=True)
    v = jnp.var(x, axis=axis, keepdims=True)
    return (x - m) / jnp.sqrt(v + eps)

def _scatter_add(tgt, idx, src, axis=0):
    return tgt.at[idx].add(src)

def _segment_sum(src, seg, n):
    return jax.ops.segment_sum(src, seg, n)
kernel_name = 'mk_gnn_resnorm_d4_gnn_r8_37c6e9'

def setup_inputs(seed: int=0):
    np.random.seed(seed)
    _w = jnp.asarray

    def _rec_inputs():
        import jax
        import jax.numpy as jnp
        _gk = jax.random.key(seed)
        x = -0.0005121 + 1.001 * jax.random.normal(jax.random.fold_in(_gk, 1), (6250, 64), jnp.float32)
        src = jax.random.randint(jax.random.fold_in(_gk, 2), (200000,), 0, 6250, jnp.int32)
        dst = jnp.minimum((6250 * jax.random.uniform(jax.random.fold_in(_gk, 3), (200000,)) ** 2.0).astype(jnp.int32), 49999)
        _o = jnp.argsort(dst, stable=True)
        src = src[_o]
        dst = dst[_o]
        return (x, src, dst)
    x, src, dst = _rec_inputs()

    def _L0_gnn_setup():
        import jax, jax.numpy as jnp
        import numpy as np
        NUM_NODES = 6250
        NUM_EDGES = 100000
        IN_CH = 64
        OUT_CH = 64
        key = jax.random.key(seed)
        k1, k2, k3, k4 = jax.random.split(key, 4)
        x = jax.random.normal(k1, (NUM_NODES, IN_CH), dtype=jnp.float32)
        edge_index = jax.random.randint(k2, (2, NUM_EDGES), 0, NUM_NODES, dtype=jnp.int32)
        W = jax.random.normal(k3, (IN_CH, OUT_CH), dtype=jnp.float32) * 0.05
        b = jax.random.normal(k4, (OUT_CH,), dtype=jnp.float32) * 0.05
        return {'x': x, 'edge_index': edge_index, 'W': W, 'b': b}
    _L0_gnn_all = _L0_gnn_setup()
    _L0_gnn_in = {k: v for k, v in _L0_gnn_all.items() if k in ('W', 'b')}
    del _L0_gnn_all

    def _L1_gnn_setup():
        import jax, jax.numpy as jnp
        import numpy as np
        N_NODES = 6250
        N_EDGES = 125000
        D_IN = 64
        D_OUT = 64
        key = jax.random.key(seed)
        kx, ks, kd, ku, kv = jax.random.split(key, 5)
        x = jax.random.normal(kx, (N_NODES, D_IN), dtype=jnp.float32)
        src = jax.random.randint(ks, (N_EDGES,), 0, N_NODES)
        dst = jax.random.randint(kd, (N_EDGES,), 0, N_NODES)
        std = float(np.sqrt(2.0 / (D_IN + D_OUT)))
        U = jax.random.normal(ku, (D_OUT, D_IN), dtype=jnp.float32) * std
        V = jax.random.normal(kv, (D_OUT, D_IN), dtype=jnp.float32) * std
        return {'x': x, 'src': src, 'dst': dst, 'U': U, 'V': V}
    _L1_gnn_all = _L1_gnn_setup()
    _L1_gnn_in = {k: v for k, v in _L1_gnn_all.items() if k in ('U', 'V')}
    del _L1_gnn_all

    def _L2_gnn_setup():
        import jax, jax.numpy as jnp
        import numpy as np
        N_NODES = 12500
        N_EDGES = 200000
        F_IN = 64
        F_OUT = 64
        key = jax.random.key(seed)
        k1, k2, k3, k4 = jax.random.split(key, 4)
        x = jax.random.normal(k1, (N_NODES, F_IN), dtype=jnp.float32)
        edge_index = jax.random.randint(k2, (2, N_EDGES), 0, N_NODES, dtype=jnp.int64)
        lim = 1.0 / np.sqrt(2 * F_IN)
        W = jax.random.uniform(k3, (F_OUT, 2 * F_IN), minval=-lim, maxval=lim, dtype=jnp.float32)
        b = jax.random.uniform(k4, (F_OUT,), minval=-lim, maxval=lim, dtype=jnp.float32)
        return {'x': x, 'edge_index': edge_index, 'num_nodes': N_NODES, 'W': W, 'b': b}
    _L2_gnn_all = _L2_gnn_setup()
    _L2_gnn_in = {k: v for k, v in _L2_gnn_all.items() if k in ('W', 'b')}
    del _L2_gnn_all

    def _L3_gnn_setup():
        import jax, jax.numpy as jnp
        import numpy as np
        N, E, D = (6250, 100000, 64)
        key = jax.random.key(seed)
        ks = jax.random.split(key, 8)
        s = 1.0 / np.sqrt(2 * D)
        inp = {'node_emb': jax.random.normal(ks[0], (N, D), dtype=jnp.float32), 'edge_index': jax.random.randint(ks[1], (2, E), 0, N, dtype=jnp.int64), 'W1': jax.random.normal(ks[2], (2 * D, D), dtype=jnp.float32) * s, 'b1': jnp.zeros((D,), dtype=jnp.float32), 'W2': jax.random.normal(ks[3], (D, D), dtype=jnp.float32) * (1.0 / np.sqrt(D)), 'b2': jnp.zeros((D,), dtype=jnp.float32), 'Wg': jax.random.normal(ks[4], (D, D), dtype=jnp.float32) * (1.0 / np.sqrt(D)), 'bg': jnp.zeros((D,), dtype=jnp.float32)}
        return inp
    _L3_gnn_all = _L3_gnn_setup()
    _L3_gnn_in = {k: v for k, v in _L3_gnn_all.items() if k in ('W1', 'b1', 'W2', 'b2', 'Wg', 'bg')}
    del _L3_gnn_all
    return {'x': x, 'src': src, 'dst': dst, 'L0_gnn_W': _L0_gnn_in['W'], 'L0_gnn_b': _L0_gnn_in['b'], 'L1_gnn_U': _L1_gnn_in['U'], 'L1_gnn_V': _L1_gnn_in['V'], 'L2_gnn_W': _L2_gnn_in['W'], 'L2_gnn_b': _L2_gnn_in['b'], 'L3_gnn_W1': _L3_gnn_in['W1'], 'L3_gnn_b1': _L3_gnn_in['b1'], 'L3_gnn_W2': _L3_gnn_in['W2'], 'L3_gnn_b2': _L3_gnn_in['b2'], 'L3_gnn_Wg': _L3_gnn_in['Wg'], 'L3_gnn_bg': _L3_gnn_in['bg']}

def reference(x, src, dst, L0_gnn_W, L0_gnn_b, L1_gnn_U, L1_gnn_V, L2_gnn_W, L2_gnn_b, L3_gnn_W1, L3_gnn_b1, L3_gnn_W2, L3_gnn_b2, L3_gnn_Wg, L3_gnn_bg):
    import jax
    import jax.numpy as jnp

    def _L0_gnn_ref(x, edge_index, W, b):
        import jax, jax.numpy as jnp
        import numpy as np
        NUM_NODES = 6250
        NUM_EDGES = 100000
        IN_CH = 64
        OUT_CH = 64
        row, col = (edge_index[0], edge_index[1])
        deg = jax.ops.segment_sum(jnp.ones_like(col, dtype=jnp.float32), col, num_segments=NUM_NODES)
        deg_inv_sqrt = jnp.where(deg > 0, (deg + 1e-16) ** (-0.5), 0.0)
        norm = deg_inv_sqrt[row] * deg_inv_sqrt[col]
        msg = norm[:, None] * x[row]
        agg = jax.ops.segment_sum(msg, col, num_segments=NUM_NODES)
        return jax.nn.relu(agg @ W + b)

    def _L1_gnn_ref(x, src, dst, U, V):
        import jax, jax.numpy as jnp
        import numpy as np
        N_NODES = 6250
        N_EDGES = 125000
        D_IN = 64
        D_OUT = 64
        agg = jax.ops.segment_sum(x[src], dst, num_segments=x.shape[0])
        out = jax.nn.relu(jnp.einsum('nd,od->no', x, U) + jnp.einsum('nd,od->no', agg, V))
        return out

    def _L2_gnn_ref(x, edge_index, num_nodes, W, b):
        import jax, jax.numpy as jnp
        import numpy as np
        N_NODES = 12500
        N_EDGES = 200000
        F_IN = 64
        F_OUT = 64
        src = edge_index[0]
        dst = edge_index[1]
        agg = jax.ops.segment_sum(x[src], dst, num_segments=num_nodes)
        deg = jax.ops.segment_sum(jnp.ones((edge_index.shape[1],), dtype=x.dtype), dst, num_segments=num_nodes)
        agg = agg / jnp.maximum(deg, 1.0)[:, None]
        h = jnp.concatenate([agg, x], axis=-1)
        out = h @ W.T + b
        return out

    def _L3_gnn_ref(node_emb, edge_index, W1, b1, W2, b2, Wg, bg):
        import jax, jax.numpy as jnp
        import numpy as np
        src, dst = (edge_index[0], edge_index[1])
        pair_emb = jnp.concatenate([node_emb[src], node_emb[dst]], axis=-1)
        h = jax.nn.relu(pair_emb @ W1 + b1)
        interaction = h @ W2 + b2
        gate = jax.nn.sigmoid(interaction @ Wg + bg)
        gated = interaction * gate
        N = node_emb.shape[0]
        summed = jax.ops.segment_sum(gated, src, num_segments=N)
        counts = jax.ops.segment_sum(jnp.ones((src.shape[0],), dtype=gated.dtype), src, num_segments=N)
        pooled = summed / jnp.maximum(counts, 1.0)[:, None]
        return pooled
    edge_index = jnp.stack([src, dst])
    x = _layernorm(x + _L0_gnn_ref(x, edge_index, L0_gnn_W, L0_gnn_b), axis=-1)
    x = _layernorm(x + _L1_gnn_ref(x, src, dst, L1_gnn_U, L1_gnn_V), axis=-1)
    x = _layernorm(x + _L2_gnn_ref(x, edge_index, 6250, L2_gnn_W, L2_gnn_b), axis=-1)
    x = _layernorm(x + _L3_gnn_ref(x, edge_index, L3_gnn_W1, L3_gnn_b1, L3_gnn_W2, L3_gnn_b2, L3_gnn_Wg, L3_gnn_bg), axis=-1)
    return x

_drawn_inputs = setup_inputs


def setup_inputs(seed=0):
    import zlib

    import numpy as np

    out = dict(_drawn_inputs(seed))
    spreads = {'L3_gnn_b1': (0.0, 0.1), 'L3_gnn_b2': (0.0, 0.1), 'L3_gnn_bg': (0.0, 0.744)}
    factors = {}
    for name, (base, spread) in spreads.items():
        noise = np.random.default_rng([zlib.crc32(name.encode()), seed]).standard_normal(out[name].shape)
        drawn = base * np.exp(spread * noise) if base else spread * noise
        out[name] = jnp.asarray(drawn.astype(out[name].dtype))
    for name, factor in factors.items():
        out[name] = (out[name] * factor).astype(out[name].dtype)
    return out
```

```python
from contextlib import ExitStack

import numpy as np

import concourse.bass as bass
from concourse import mybir
from concourse.alu_op_type import AluOpType as ALU

ACT = mybir.ActivationFunctionType
F32 = mybir.dt.float32
BF16 = mybir.dt.bfloat16
I32 = mybir.dt.int32
AX_X = mybir.AxisListType.X

P = 128
NODES = 6250
EDGES = 200000
D = 64
EPS = 1e-5

NT = -(-NODES // P)
NTP = NT + NT % 2
EG = -(-NTP // 8)
FULL = NODES // P
REST = NODES - FULL * P

ID_BITS = 13
LOG = 18
COLS = (1 << LOG) // P
COL_BITS = LOG - 7
ONE_BITS = 0x40000000
KEY_MASK = (1 << (2 * ID_BITS)) - 1
SENTINEL = float(np.uint32(ONE_BITS | KEY_MASK).view(np.float32))
EP = 125
EC = EDGES // EP
assert EP * EC == EDGES and EDGES < 1 << LOG and NODES < 1 << ID_BITS

LEVELS = 3
MCOLS = NT * P
CUT = [0, -(-NT // 2), NT]
MTILES = LEVELS * NT + 1
SKIP = 1 << 30
SC = 16
CHUNKS = -(-EDGES // (P * 2 * SC)) * 2 * SC
ROUNDS = CHUNKS // SC
HB = 8

G = 4
GROUPS = -(-EDGES // (P * G))
ITEMS = GROUPS + NT - 1
ITEMS += (-ITEMS) % 4
IC = ITEMS * G
ICB = -(-IC // P)

SORT_X, SORT_Y = "x", "y"


def sort_plan():
    steps, cur = [], 0

    def add(kind, **how):
        nonlocal cur
        steps.append(dict(how, kind=kind, src=cur, dst=1 - cur))
        cur = 1 - cur

    def col(bit):
        return bit - COL_BITS if bit >= COL_BITS else bit

    for k in range(1, COL_BITS):
        for j in range(k - 1, -1, -1):
            add("stage", stride=j, direction=k, unflip=False)
    add("sign", bit=COL_BITS)
    for j in range(COL_BITS - 1, -1, -1):
        add("stage", stride=j, direction=None, unflip=False)
    for k in range(COL_BITS + 1, LOG + 1):
        add("turn", bit=None)
        for j in range(k - 1, 6, -1):
            add("stage", stride=col(j), direction=col(k) if k < LOG else None, unflip=(j == k - 1))
        add("turn", bit=k if k < LOG else None)
        for j in range(6, -1, -1):
            add("stage", stride=j, direction=None, unflip=False)
    return steps


def build_gnn(nc, x_in, src_in, dst_in, w0, b0, u1, v1, w2l, b2l, w1, b1, w2, b2, wg, bg, out):
    plan = sort_plan()
    turns = [n for n, s in enumerate(plan) if s["kind"] == "turn"]
    last = len(plan)

    adj = nc.dram_tensor("adjacency", [MTILES * P, MCOLS], BF16).ap()
    adj_cells = adj.rearrange("a (b o) -> (a b) o", o=1)
    b_table = nc.dram_tensor("b_table", [NTP * P, D], F32).ap()
    src_rows = nc.dram_tensor("src_rows", [ICB * P, P], BF16).ap()

    with ExitStack() as ctx:
        def sb(name, shape, dt):
            return ctx.enter_context(nc.sbuf_tensor(name, shape, dt))

        def sem(name):
            return ctx.enter_context(nc.semaphore(name))

        ident = sb("ident", [P, P], F32)
        iota_i = sb("iota_i", [P, P], I32)
        iota_f = sb("iota_f", [P, P], F32)
        iota_b = sb("iota_b", [P, P], BF16)
        part_i = sb("part_i", [P, 8], I32)
        part_f = sb("part_f", [P, 1], F32)
        sign = sb("sign", [P, 7], F32)
        ones = sb("ones", [P, 1], F32)
        t128 = sb("t128", [P, NTP], F32)
        item_i = sb("item_i", [NT, ITEMS], I32)

        wb = sb("wb", [P, 7, P], F32)
        wt = sb("wt", [P, 4, P], F32)
        w2cat = sb("w2cat", [D + 1, 2 * D], F32)
        w2t = sb("w2t", [D, D + 1], F32)
        wg_sb = sb("wg_sb", [D, D], F32)
        bg_sb = sb("bg_sb", [D + 1, D], F32)
        bias = sb("bias", [P, 2, D], F32)
        b1col = sb("b1col", [D, 1], F32)

        x3 = sb("x3", [P, LEVELS * NT + 1, 3 * D], BF16)
        region = x3[:].rearrange("p a b -> p (a b)").bitcast(F32)

        def part(n):
            return region[:, n * COLS:(n + 1) * COLS]

        keys = [part(0), part(1)]
        same, runs, sorted_y, runs_y = part(2), part(3), part(4), part(5)
        src_ld, dst_ld = part(2).bitcast(I32)[0:EP, 0:EC], part(3).bitcast(I32)[0:EP, 0:EC]

        rows = sb("rows", [P, 4, CUT[1] * P], BF16)
        rflat = rows[:].rearrange("p a b -> p (a b)")
        hot = rflat[:, 0:2 * 2 * HB * 2 * P].rearrange("p (r w c n) -> p r w c n", r=2, w=4, c=HB)

        cell = sb("cell", [P, LEVELS, CHUNKS], I32)
        digit = sb("digit", [P, LEVELS, CHUNKS], BF16)
        cell_r = sb("cell_r", [P, 2, SC], I32)
        digit_r = sb("digit_r", [P, 2, SC], BF16)
        dst_i = sb("dst_i", [P, CHUNKS], I32)
        src_f = sb("src_f", [P, CHUNKS], F32)
        halves = sb("halves", [P, 4, CHUNKS], BF16)

        X = sb("X", [P, NTP, D], F32)
        AGG = sb("AGG", [P, NTP, D], F32)
        T1 = sb("T1", [P, NTP, D], F32)
        T2 = AGG
        zero = T1[:].rearrange("p a b -> p (a b)").bitcast(BF16)[:, 0:MCOLS]
        tmp_i = AGG[:].rearrange("p a b -> p (a b)").bitcast(I32)[:, 0:CHUNKS]
        tmp_f = AGG[:].rearrange("p a b -> p (a b)")[:, CHUNKS:2 * CHUNKS]
        tmp_g = rflat.bitcast(F32)[:, 0:CHUNKS]
        aggT = sb("aggT", [P, 2, 512], F32)
        xT = sb("xT", [P, 512], F32)

        small = sb("small", [P, 16], F32)
        srow = sb("srow", [1, 8, 132], F32)
        deg = sb("deg", [P, 2, NT], F32)
        scale = sb("scale", [P, 4, NTP], F32)
        stat = sb("stat", [P, 3, NTP], F32)
        ctl = sb("ctl", [1, 4], I32)
        item_cmp = sb("item_cmp", [NT, ITEMS], F32)
        tile_tab = sb("tile_tab", [1, ITEMS + 4], I32)
        chunk_tab = sb("chunk_tab", [1, ITEMS], I32)
        dst_items = sb("dst_items", [P, IC], I32)
        src_items = halves[:].rearrange("p a b -> p (a b)").bitcast(F32)[:, 0:ICB * P]

        spare = x3[:].rearrange("p a b -> p (a b)")[:, NTP * 3 * D:]
        at = 0

        def ring(count, size, dt):
            nonlocal at
            n = count * size * (2 if dt == F32 else 1)
            v = spare[:, at:at + n]
            at += n
            return (v.bitcast(F32) if dt == F32 else v).rearrange("p (s n) -> p s n", s=count)

        BGT = ring(4, G * D, F32).rearrange("p s (j f) -> p s j f", j=G)
        SROW = ring(4, G * P, BF16)
        OT = ring(2, G * P, BF16)
        OS = ring(4, G * P, F32).rearrange("p s (j n) -> p s j n", j=G)
        SG = ring(2, G * D, F32).rearrange("p s (j f) -> p s j f", j=G)
        MG = ring(2, G * D, F32).rearrange("p s (j f) -> p s j f", j=G)
        H = ring(2, G * P, F32)
        AT = sb("AT", [P, 2, 3 * D], BF16)
        srct = sb("srct", [P, 2, P], BF16)
        gidx = sb("gidx", [P, 4, G], I32)

        ps = ctx.enter_context(nc.psum_tensor("ps", [P, 8, 512], F32))
        psf = ps[:].rearrange("p b n -> p (b n)")
        turn_ps = psf[:, 0:COLS]
        acc_ps = psf[:, 0:NT * D].rearrange("p (t f) -> p t f", f=D)

        edges_in = sem("edges_in")
        x_landed = sem("x_landed")
        weights_in = sem("weights_in")
        consts = sem("consts")
        pool_passed = sem("pool_passed")
        dve = sem("dve")
        edge_rows = sem("edge_rows")
        carry_cols = sem("carry_cols")
        y_turned = sem("y_turned")
        longest_row = sem("longest_row")
        counted = sem("counted")
        tile_counts = sem("tile_counts")
        last_item_col = sem("last_item_col")
        item_tiles = sem("item_tiles")
        deg_root = sem("deg_root")
        weights_turned = sem("weights_turned")
        agg_turned = sem("agg_turned")
        x_turned = sem("x_turned")
        aggT_copied = sem("aggT_copied")
        product = sem("product")
        root_ready = sem("root_ready")
        pair_turned = sem("pair_turned")
        pair_product = sem("pair_product")
        fill_done = sem("fill_done")
        weights_copied = sem("weights_copied")
        gate_weights = sem("gate_weights")
        gidx_ready = sem("gidx_ready")
        src_turned = sem("src_turned")
        src_turned_copied = sem("src_turned_copied")
        sorted_step = sem("sorted_step")
        turned = sem("turned")
        turn_out = sem("turn_out")
        zeroed = sem("zeroed")
        cells_ready = sem("cells_ready")
        cells_kept = sem("cells_kept")
        stored = [sem("stored0"), sem("stored1")]
        hot_ready = sem("hot_ready")
        hot_used = sem("hot_used")
        items_ready = sem("items_ready")
        item_copied = sem("item_copied")
        rows_landed = [sem(f"rows_landed{n}") for n in range(4)]
        rows_free = sem("rows_free")
        split_ready = sem("split_ready")
        agg_ready = sem("agg_ready")
        table_out = sem("table_out")
        srows_out = [sem("srows_out0"), sem("srows_out1")]
        srow_landed = [sem(f"srow_landed{n}") for n in range(4)]
        b_landed = [sem(f"b_landed{n}") for n in range(4)]
        b_free = sem("b_free")
        at_ready = sem("at_ready")
        ot_ready = sem("ot_ready")
        os_ready = sem("os_ready")
        h_ps_ready = sem("h_ps_ready")
        h_ready = sem("h_ready")
        g_ps_ready = sem("g_ps_ready")
        gate_ready = sem("gate_ready")
        gated_ready = sem("gated_ready")
        sum_ready = sem("sum_ready")
        sum_taken = sem("sum_taken")
        stored_out = sem("stored_out")

        mark = {}

        class Seq:

            def __init__(self, eng, s):
                self.eng, self.s, self.n = eng, s, 0

            def done(self, ins):
                self.n += 1
                ins.then_inc(self.s, 1)
                return self.n

            def link(self, ins):
                self.done(ins)
                self.eng.wait_ge(self.s, self.n)

            def mark(self, name, ins):
                mark[name] = self.done(ins)

        block = ctx.enter_context(nc.Block())

        def scan_ap(col, n):
            return col.to_broadcast([col.shape[0], n])

        def over_f(v):
            return v.unsqueeze(2).to_broadcast([P, v.shape[1], D])

        @block.vector
        def _(e):
            q = Seq(e, dve)
            e.wait_ge(consts, 12)
            for b in range(7):
                ins = e.tensor_scalar(part_i[:, b:b + 1], part_i[:, b:b + 1], b, 1,
                                      ALU.logical_shift_right, ALU.bitwise_and)
            q.link(ins)
            q.link(e.tensor_copy(sign[:], part_i[:, 0:7]))
            q.link(e.tensor_scalar(sign[:], sign[:], -2.0, 1.0, ALU.mult, ALU.add))
            q.done(e.tensor_copy(iota_f[:], iota_i[:]))
            q.done(e.tensor_copy(iota_b[:], iota_i[:]))
            q.done(e.tensor_copy(part_f[:], part_i[:, 7:8]))
            q.done(e.tensor_scalar(t128[:], iota_i[:, 0:NTP], -float(P), None, ALU.mult))
            mark["consts_dve"] = q.n

            e.wait_ge(edges_in, 32)
            q.link(e.tensor_scalar(src_ld, src_ld, ID_BITS, ONE_BITS, ALU.logical_shift_left, ALU.bitwise_or))
            k_i = keys[0].bitcast(I32)
            q.link(e.tensor_tensor(k_i[0:EP, 0:EC], src_ld, dst_ld, ALU.bitwise_or))

            e.wait_ge(gate_weights, 1)
            q.done(e.tensor_tensor(w2cat[:, D:2 * D], ps[0:D + 1, 6, D:2 * D], bg_sb[:], ALU.add))

            n_turn = 0
            for n, s in enumerate(plan):
                if n:
                    e.wait_ge(sorted_step, n)
                if n and plan[n - 1]["kind"] == "turn":
                    e.wait_ge(turn_out, n_turn)
                a, b = keys[s["src"]], keys[s["dst"]]
                if s["kind"] == "sign":
                    c = s["bit"] - COL_BITS
                    ins = e.tensor_scalar(b, a, sign[:, c:c + 1], None, ALU.mult)
                elif s["kind"] == "turn":
                    for bank in (1, 3):
                        e.wait_ge(turned, 4 * n_turn + bank + 1)
                        r = slice(bank * 512, bank * 512 + 512)
                        if s["bit"] is None:
                            ins = e.tensor_copy(b[:, r], turn_ps[:, r])
                        else:
                            c = s["bit"] - COL_BITS
                            ins = e.tensor_scalar(b[:, r], turn_ps[:, r], sign[:, c:c + 1], None, ALU.mult)
                    n_turn += 1
                else:
                    cj, ck = s["stride"], s["direction"]

                    def view(t, high, down):
                        if ck is None:
                            return t.rearrange("p (a t c) -> p a t c", t=2, c=1 << cj)[:, :, high, :]
                        lo, hi = min(cj, ck), max(cj, ck)
                        w = t.rearrange("p (a t b u c) -> p a t b u c", t=2, u=2, c=1 << lo,
                                        b=1 << (hi - lo - 1))
                        return w[:, :, down, :, high, :] if ck > cj else w[:, :, high, :, down, :]

                    for down in ((0,) if ck is None else (0, 1)):
                        for high in (0, 1):
                            op = ALU.min if high == down else ALU.max
                            if s["unflip"]:
                                ins = e.scalar_tensor_tensor(out=view(b, high, down), in0=view(a, 1, down),
                                                             scalar=-1.0, in1=view(a, 0, down),
                                                             op0=ALU.mult, op1=op)
                            else:
                                ins = e.tensor_tensor(view(b, high, down), view(a, 0, down),
                                                      view(a, 1, down), op)
                ins.then_inc(sorted_step, 1)
            e.wait_ge(sorted_step, last)

            S = keys[last % 2]
            q.done(e.memset(same[:, 0:1], 0.0))
            q.link(e.tensor_tensor(same[:, 1:COLS], S[:, 1:COLS], S[:, 0:COLS - 1], ALU.is_equal))
            q.link(e.tensor_tensor_scan(runs, same, scan_ap(ones[:], COLS), 0.0, ALU.mult, ALU.add))
            q.done(e.tensor_copy(small[:, 0:1], S[:, 0:1]))
            q.done(e.tensor_copy(small[:, 1:2], S[:, COLS - 1:COLS]))
            q.mark("edge_cols", e.tensor_copy(small[:, 2:3], runs[:, COLS - 1:COLS]))
            e.wait_ge(edge_rows, 1)
            r_first, r_last, r_run = (srow[0:1, n, 0:P] for n in range(3))
            q.link(e.tensor_copy(srow[0:1, 0:3, 0:P], ps[0:1, 4, 0:3 * P].rearrange("p (a b) -> p a b", a=3)))
            joins = srow[0:1, 3, 0:P + 1]
            q.done(e.memset(srow[0:1, 3:8, :], 0.0))
            e.wait_ge(dve, q.n)
            q.link(e.tensor_tensor(joins[:, 1:P], r_first[:, 1:P], r_last[:, 0:P - 1], ALU.is_equal))
            q.done(e.scalar_tensor_tensor(out=srow[0:1, 4, 1:P], in0=r_run[:, 0:P - 1], scalar=float(COLS),
                                          in1=joins[:, 1:P], op0=ALU.is_equal, op1=ALU.mult))
            q.done(e.tensor_tensor(srow[0:1, 5, 1:P], r_run[:, 0:P - 1], joins[:, 1:P], ALU.mult))
            q.done(e.tensor_scalar(srow[0:1, 7, 0:P], joins[:, 1:P + 1], -1.0, 1.0, ALU.mult, ALU.add))
            e.wait_ge(dve, q.n)
            q.mark("carry_row", e.tensor_tensor_scan(srow[0:1, 6, 0:P], srow[0:1, 4, 0:P], srow[0:1, 5, 0:P],
                                                     0.0, ALU.mult, ALU.add))
            e.wait_ge(carry_cols, 1)
            q.done(e.tensor_copy(small[:, 4:6], ps[:, 4, 0:2]))
            q.done(e.memset(same[:, 0:1], 1.0))
            e.wait_ge(dve, q.n)
            q.link(e.tensor_tensor_scan(runs, same, scan_ap(ones[:], COLS), small[:, 4:5], ALU.mult, ALU.add))
            run_end = keys[1 - last % 2]
            q.done(e.scalar_tensor_tensor(out=run_end[:, 0:COLS - 1], in0=same[:, 1:COLS], scalar=0.0,
                                          in1=runs[:, 0:COLS - 1], op0=ALU.is_equal, op1=ALU.mult))
            q.mark("run_ends", e.tensor_tensor(run_end[:, COLS - 1:COLS], runs[:, COLS - 1:COLS],
                                               small[:, 5:6], ALU.mult))

            for n, dest in enumerate((sorted_y, runs_y)):
                d = dest.rearrange("p (h m) -> p m h", m=16)
                for bank in range(4):
                    e.wait_ge(y_turned, 4 * n + bank + 1)
                    q.done(e.tensor_copy(d[:, 4 * bank:4 * bank + 4, :],
                                         ps[:, bank, :].rearrange("p (m h) -> p m h", m=4)))
                mark[f"turn_y{n}"] = q.n
            e.wait_ge(dve, q.n)
            K = tmp_i
            q.link(e.tensor_scalar(K, sorted_y.bitcast(I32)[:, 0:CHUNKS], KEY_MASK, None, ALU.bitwise_and))
            I = keys[0].bitcast(I32)[:, 0:CHUNKS]
            J = keys[1].bitcast(I32)[:, 0:CHUNKS]
            for w, (sh, m) in enumerate(((0, 127), (7, 63), (ID_BITS, 127), (ID_BITS + 7, 63))):
                t = (I, J)[w % 2]
                q.link(e.tensor_scalar(t, K, sh, m, ALU.logical_shift_right, ALU.bitwise_and))
                q.done(e.tensor_copy(halves[:, w, :], t))
            q.link(e.tensor_scalar(same.bitcast(I32)[:, 0:CHUNKS], K, ID_BITS, None, ALU.logical_shift_right))
            q.done(e.tensor_copy(src_f[:], same.bitcast(I32)[:, 0:CHUNKS]))
            q.link(e.tensor_scalar(runs.bitcast(I32)[:, 0:CHUNKS], K, (1 << ID_BITS) - 1, None, ALU.bitwise_and))
            q.done(e.tensor_scalar(dst_i[:], runs.bitcast(I32)[:, 0:CHUNKS], NTP * P - 1, None, ALU.min))
            q.link(e.scalar_tensor_tensor(out=tmp_f, in0=halves[:, 3, :], scalar=float(NT),
                                          in1=runs_y[:, 0:CHUNKS], op0=ALU.is_lt, op1=ALU.mult))
            q.done(e.tensor_reduce(small[:, 6:7], tmp_f, AX_X, ALU.max))
            mark["max_run"] = q.n
            q.done(e.tensor_copy(I, tmp_f))
            q.done(e.tensor_scalar(J, tmp_f, 0.0, float(SKIP), ALU.is_equal, ALU.mult))
            e.wait_ge(dve, q.n)
            q.link(e.tensor_scalar(K, K, P - 1, None, ALU.bitwise_and))
            q.link(e.tensor_tensor(J, K, J, ALU.bitwise_or))
            S2, S3 = same.bitcast(I32)[:, 0:CHUNKS], K
            for lev in range(LEVELS):
                q.link(e.tensor_scalar(S2, I, 8 * lev, 255, ALU.logical_shift_right, ALU.bitwise_and))
                q.link(e.tensor_copy(digit[:, lev, :], S2))
                q.link(e.tensor_scalar(S2, src_f[:], float(NT * P * lev), float(NT), ALU.add, ALU.mult))
                q.link(e.tensor_tensor(S3, S2, halves[:, 1, :], ALU.add))
                q.link(e.tensor_scalar(S3, S3, 7, None, ALU.logical_shift_left))
                q.link(e.tensor_tensor(cell[:, lev, :], S3, J, ALU.bitwise_or))
            e.wait_ge(longest_row, 1)
            q.link(e.tensor_reduce(srow[0:1, 0, 0:1], ps[0:1, 4, 128:256], AX_X, ALU.max))
            many = srow[0:1, 0, 1:2]
            q.link(e.tensor_scalar(many, srow[0:1, 0, 0:1], 255.0, None, ALU.is_gt))
            one_level = ((NT + 1) // 2, NT + 1, ROUNDS // 2)
            all_levels = (MTILES // 2, MTILES, LEVELS * ROUNDS // 2)
            for c, (few, lots) in enumerate(zip(one_level, all_levels)):
                q.done(e.tensor_scalar(ctl[0:1, c:c + 1], many, float(lots - few), float(few), ALU.mult, ALU.add))
            mark["ctl"] = q.n

            def one_hots(half, c0, first):
                for w in range(4):
                    width = P if w % 2 == 0 else NT
                    ids = halves[:, w, bass.ds(c0, HB)].unsqueeze(2).to_broadcast([P, HB, width])
                    row = iota_b[:, 0:width].unsqueeze(1).to_broadcast([P, HB, width])
                    ins = e.tensor_tensor(hot[:, half, w, :, 0:width], row, ids, ALU.is_equal)
                return ins

            q.done(e.memset(ps[:, 7, :], 0.0))
            e.wait_ge(dve, q.n)
            mark["count_start"] = q.n
            with e.Fori(0, CHUNKS // (2 * HB)) as it:
                for half in range(2):
                    e.wait_ge(hot_used, 2 * it + half + 1)
                    one_hots(half, (2 * it + half) * HB, None).then_inc(hot_ready, 1)

            e.wait_ge(counted, 1)
            q.link(e.tensor_copy(deg[:], ps[:, 7, 0:128].rearrange("p (a b) -> p a b", a=2)[:, :, 0:NT]))
            mark["deg"] = q.n
            q.done(e.memset(src_items[:, IC:], 0.0))
            q.done(e.memset(scale[:], 0.0))
            q.done(e.tensor_scalar(stat[:, 0:2, 0:NT], deg[:], 1.0, None, ALU.max))
            e.wait_ge(dve, q.n)
            q.done(e.reciprocal(scale[:, 1:3, 0:NT], stat[:, 0:2, 0:NT]))
            q.mark("deg_plus", e.tensor_scalar(stat[:, 2, 0:NT], deg[:, 0, :], 1e-16, None, ALU.add))
            e.wait_ge(tile_counts, 1)
            q.link(e.tensor_copy(srow[0:1, 1, 0:NT], ps[0:1, 7, 128:128 + NT]))
            q.link(e.tensor_tensor_scan(srow[0:1, 2, 0:NT], scan_ap(ones[0:1, :], NT), srow[0:1, 1, 0:NT],
                                        0.0, ALU.mult, ALU.add))
            tile_ends = tile_tab[0:1, 0:NT]
            q.link(e.tensor_copy(tile_ends, srow[0:1, 2, 0:NT]))
            q.link(e.tensor_scalar(tile_ends, tile_ends, 9, None, ALU.logical_shift_right))
            q.link(e.tensor_copy(srow[0:1, 3, 0:NT], tile_ends))
            q.mark("last_items", e.tensor_tensor(srow[0:1, 4, 0:NT], srow[0:1, 3, 0:NT], iota_f[0:1, 0:NT], ALU.add))
            e.wait_ge(last_item_col, 1)
            q.link(e.tensor_copy(small[0:NT, 8:9], ps[0:NT, 7, 192:193]))
            q.mark("item_cmp", e.tensor_scalar(item_cmp[:], item_i[:], small[0:NT, 8:9], None, ALU.is_gt))
            e.wait_ge(item_tiles, 1)
            q.link(e.tensor_copy(tile_tab[0:1, 0:ITEMS], ps[0:1, 6, 0:ITEMS]))
            q.link(e.tensor_tensor(chunk_tab[:], item_i[0:1, :], tile_tab[0:1, 0:ITEMS], ALU.subtract))
            q.done(e.tensor_scalar(chunk_tab[:], chunk_tab[:], float(G), None, ALU.mult))
            mark["items"] = q.n

            e.wait_ge(deg_root, 1)
            q.link(e.tensor_scalar(scale[:, 3, 0:NT], deg[:, 0, :], 0.0, None, ALU.is_gt))
            q.link(e.reciprocal(stat[:, 1, 0:NT], stat[:, 0, 0:NT]))
            q.link(e.tensor_tensor(scale[:, 0, 0:NT], stat[:, 1, 0:NT], scale[:, 3, 0:NT], ALU.mult))

            def split(v, rest):
                q.link(e.tensor_copy(x3[:, 0:NTP, 0:D], v))
                q.link(e.tensor_tensor(rest, v, x3[:, 0:NTP, 0:D], ALU.subtract))
                q.link(e.tensor_copy(x3[:, 0:NTP, D:2 * D], rest))
                q.link(e.tensor_tensor(rest, rest, x3[:, 0:NTP, D:2 * D], ALU.subtract))
                q.link(e.tensor_copy(x3[:, 0:NTP, 2 * D:], rest))

            def layernorm():
                q.link(e.tensor_reduce(stat[:, 0, :], X[:], AX_X, ALU.add))
                q.link(e.tensor_scalar(stat[:, 0, :], stat[:, 0, :], -1.0 / D, None, ALU.mult))
                q.link(e.tensor_tensor(X[:], X[:], over_f(stat[:, 0, :]), ALU.add))
                q.link(e.tensor_tensor(T1[:], X[:], X[:], ALU.mult))
                q.link(e.tensor_reduce(stat[:, 1, :], T1[:], AX_X, ALU.add))
                return q.done(e.tensor_scalar(stat[:, 1, :], stat[:, 1, :], 1.0 / D, EPS, ALU.mult, ALU.add))

            def normalise(n):
                e.wait_ge(root_ready, n)
                q.link(e.reciprocal(stat[:, 0, :], stat[:, 2, :]))
                q.link(e.tensor_tensor(X[:], X[:], over_f(stat[:, 0, :]), ALU.mult))

            e.wait_ge(x_landed, 32)
            e.wait_ge(fill_done, 1)
            for layer in range(3):
                if layer == 0:
                    q.link(e.tensor_tensor(T1[:], X[:], over_f(scale[:, 0, :]), ALU.mult))
                    split(T1[:], AGG[:])
                else:
                    split(X[:], AGG[:])
                for lev in range(1, LEVELS):
                    q.done(e.tensor_scalar(x3[:, lev * NT:(lev + 1) * NT, :], x3[:, 0:NT, :],
                                           float(256 ** lev), None, ALU.mult))
                q.done(e.memset(x3[:, LEVELS * NT, :], 0.0))
                if layer == 1:
                    e.wait_ge(src_turned_copied, ICB)
                q.done(e.memset(psf[:, 0:7 * 512], 0.0))
                mark[f"split{layer}"] = q.n
                e.wait_ge(agg_ready, layer + 1)
                if layer == 1:
                    q.done(e.tensor_copy(AGG[:, 0:NT, :], acc_ps))
                else:
                    sc = scale[:, 0 if layer == 0 else 1, 0:NT]
                    q.done(e.tensor_tensor(AGG[:, 0:NT, :], acc_ps, over_f(sc), ALU.mult))
                q.done(e.memset(AGG[:, NT:NTP, :], 0.0))
                mark[f"agg{layer}"] = q.n
                e.wait_ge(dve, q.n)
                for g in range(EG):
                    t0, t1 = 8 * g, min(8 * g + 8, NTP)
                    w = (t1 - t0) * D
                    n = layer * EG + g
                    if layer:
                        e.wait_ge(x_turned, n - EG + 1)
                        q.mark(f"xT{layer}_{g}", e.tensor_copy(xT[:, 0:w], ps[:, 2 + g % 2, 0:w]))
                    e.wait_ge(product, n + 1)
                    o = ps[:, 4 + g % 2, 0:w].rearrange("p (t f) -> p t f", f=D)
                    xs = X[:, t0:t1, :]
                    if layer == 1:
                        q.done(e.scalar_tensor_tensor(out=xs, in0=o, scalar=0.0, in1=xs, op0=ALU.max, op1=ALU.add))
                    else:
                        bb = bias[:, layer // 2, :].unsqueeze(1).to_broadcast([P, t1 - t0, D])
                        q.link(e.tensor_tensor(T1[:, t0:t1, :], o, bb, ALU.add))
                        if layer == 0:
                            q.done(e.scalar_tensor_tensor(out=xs, in0=T1[:, t0:t1, :], scalar=0.0, in1=xs,
                                                          op0=ALU.max, op1=ALU.add))
                        else:
                            q.done(e.tensor_tensor(xs, T1[:, t0:t1, :], xs, ALU.add))
                    mark[f"out{layer}_{g}"] = q.n
                e.wait_ge(dve, q.n)
                mark[f"var{layer}"] = layernorm()
                normalise(layer + 1)
                mark[f"x{layer}"] = q.n

            for g in range(EG):
                t0, t1 = 8 * g, min(8 * g + 8, NTP)
                w = (t1 - t0) * D
                e.wait_ge(pair_turned, g + 1)
                q.mark(f"pT_{g}", e.tensor_copy(xT[:, 0:w], ps[:, g % 2, 0:w]))
                e.wait_ge(pair_product, g + 1)
                q.done(e.tensor_copy(T1[:, t0:t1, :], ps[:, 2 + g % 2, 0:w].rearrange("p (t f) -> p t f", f=D)))
                q.mark(f"p_{g}", e.tensor_copy(AGG[:, t0:t1, :],
                                               ps[:, 4 + g % 2, 0:w].rearrange("p (t f) -> p t f", f=D)))
            e.wait_ge(dve, q.n)
            mark["b_rows"] = q.n
            e.wait_ge(table_out, 16)
            split(T1[:], AGG[:])
            q.done(e.memset(AGG[:], 0.0))
            q.done(e.memset(H[D:D + 1, :, :], 1.0))
            e.wait_ge(dve, q.n)
            mark["a_split"] = q.n

            def make_hot_t(i, rnd, s, first):
                e.wait_ge(srow_landed[s], 16 * rnd + 16)
                if not first:
                    e.wait_ge(h_ps_ready, i - 1)
                e.tensor_scalar(OT[:, s % 2, :], SROW[:, s, :], part_f[:, 0:1], None,
                                ALU.is_equal).then_inc(ot_ready, 1)

            def make_hot(i, s, first):
                if not first:
                    e.wait_ge(sum_ready, i - 3)
                for j in range(G):
                    ins = e.tensor_scalar(OS[:, s, j, :], iota_f[:], src_items[:, bass.ds(G * i + j, 1)],
                                          None, ALU.is_equal)
                ins.then_inc(os_ready, 1)

            def gated(i, u, first):
                e.wait_ge(gate_ready, i + 1)
                if not first:
                    e.wait_ge(sum_ready, i - 1)
                e.tensor_tensor(MG[:, u, :, :], SG[:, u, :, :],
                                ps[:, 2 + u, :].rearrange("p (j f) -> p j f", j=G)[:, :, 0:D],
                                ALU.mult).then_inc(gated_ready, 1)

            def add_sum(i, u):
                tile_reg = e.snap(e.value_load(tile_tab[0:1, bass.ds(i, 1)], min_val=0, max_val=NTP - 1))
                e.wait_ge(sum_ready, i + 1)
                e.wait_ge(sum_taken, i + 1)
                a = AGG[:, bass.ds(tile_reg, 1), :].rearrange("p a f -> p (a f)")
                e.tensor_tensor(a, a, ps[:, 4 + u, 0:D], ALU.add).then_inc(sum_taken, 1)

            e.sem_inc(sum_taken, 1)
            for i in range(4):
                make_hot_t(i, 0, i, i < 2)
                if i >= 2:
                    gated(i - 2, i % 2, i < 4)
                if i >= 3:
                    add_sum(i - 3, (i - 3) % 2)
                make_hot(i, i, True)
            with e.Fori(1, ITEMS // 4) as r:
                for s in range(4):
                    i = 4 * r + s
                    make_hot_t(i, r, s, False)
                    gated(i - 2, s % 2, False)
                    add_sum(i - 3, (s + 1) % 2)
                    make_hot(i, s, False)
            for i in (ITEMS - 2, ITEMS - 1):
                gated(i, i % 2, False)
            for i in range(ITEMS - 3, ITEMS):
                add_sum(i, i % 2)
            e.wait_ge(sum_taken, ITEMS + 1)
            q.link(e.tensor_tensor(AGG[:], AGG[:], over_f(scale[:, 2, :]), ALU.mult))
            q.link(e.tensor_tensor(X[:], X[:], AGG[:], ALU.add))
            mark["var3"] = layernorm()
            normalise(4)
            mark["final"] = q.n

        @block.gpsimd
        def _(e):
            def const(ins):
                ins.then_inc(consts, 1)

            const(e.memset(ident[:], 0.0))
            const(e.memset(ones[:], 1.0))
            const(e.memset(T1[:], 0.0))
            const(e.memset(X[:], 0.0))
            const(e.memset(wb[:], 0.0))
            const(e.memset(bg_sb[:], 0.0))
            const(e.memset(keys[0], SENTINEL))
            const(e.memset(tile_tab[:], 0.0))
            const(e.iota(iota_i[:], pattern=[[1, P]], base=0, channel_multiplier=0))
            const(e.iota(part_i[:], pattern=[[0, 8]], base=0, channel_multiplier=1))
            const(e.iota(item_i[:], pattern=[[1, ITEMS]], base=0, channel_multiplier=0))
            e.wait_ge(consts, 11)
            const(e.affine_select(out=ident[:], in_=ident[:], compare_op=ALU.not_equal, fill=1.0, base=0,
                                  pattern=[[-1, P]], channel_multiplier=1))

            e.wait_ge(dve, mark["ctl"])
            n_pairs = e.snap(e.value_load(ctl[0:1, 2:3], min_val=ROUNDS // 2, max_val=LEVELS * ROUNDS // 2))
            e.wait_ge(fill_done, 1)
            cells = cell[:].rearrange("p a b -> p (a b)")
            digits = digit[:].rearrange("p a b -> p (a b)")

            def store_round(pair, h, first):
                c0 = (2 * pair + h) * SC
                if not first:
                    e.wait_ge(stored[h], 16 * SC * pair)
                e.tensor_copy(cell_r[:, h, :], cells[:, bass.ds(c0, SC)]).then_inc(cells_kept, 1)
                e.tensor_copy(digit_r[:, h, :], digits[:, bass.ds(c0, SC)]).then_inc(cells_kept, 1)
                e.wait_ge(cells_kept, 4 * pair + 2 * h + 2)
                e.sem_inc(pool_passed, 1)
                for c in range(SC):
                    e.indirect_dma_start(
                        out=adj_cells, out_offset=bass.IndirectOffsetOnAxis(ap=cell_r[:, h, c:c + 1], axis=0),
                        in_=digit_r[:, h, c:c + 1], in_offset=None,
                        bounds_check=MTILES * P * MCOLS - 1, oob_is_err=False).then_inc(stored[h], 16)

            for h in range(2):
                store_round(0, h, True)
            with e.Fori(1, n_pairs) as pair:
                for h in range(2):
                    store_round(pair, h, False)
            for h in range(2):
                e.wait_ge(stored[h], 16 * SC * n_pairs)
                e.sem_inc(pool_passed, 1)
            e.sem_inc(cells_ready, 1)

            e.wait_ge(table_out, 16)
            e.wait_ge(dve, mark["a_split"])

            def gather_item(rnd, s, first):
                i = 4 * rnd + s
                if not first:
                    e.wait_ge(b_landed[s], 16 * G * rnd)
                e.tensor_copy(gidx[:, s, :], dst_items[:, bass.ds(G * i, G)]).then_inc(gidx_ready, 1)
                if not first:
                    e.wait_ge(h_ps_ready, i - 3)
                e.wait_ge(gidx_ready, i + 1)
                e.sem_inc(pool_passed, 1)
                for j in range(G):
                    e.indirect_dma_start(
                        out=BGT[:, s, j, :], out_offset=None, in_=b_table,
                        in_offset=bass.IndirectOffsetOnAxis(ap=gidx[:, s, j:j + 1], axis=0)
                    ).then_inc(b_landed[s], 16)

            for s in range(4):
                gather_item(0, s, True)
            with e.Fori(1, ITEMS // 4) as rnd:
                for s in range(4):
                    gather_item(rnd, s, False)
            for s in range(4):
                e.wait_ge(b_landed[s], 4 * G * ITEMS)

        @block.sync
        def _(e):
            e.dma_start(src_ld, src_in.rearrange("(p n) -> p n", p=EP)).then_inc(edges_in, 16)
            e.dma_start(dst_ld, dst_in.rearrange("(p n) -> p n", p=EP)).then_inc(edges_in, 16)
            e.wait_ge(consts, 11)
            diag = [w0, u1, v1, w2l[:, 0:D], w2l[:, D:2 * D], w1[0:D, :], w1[D:2 * D, :]]
            for n, w in enumerate(diag):
                for h in range(2):
                    e.dma_start(wb[h * D:(h + 1) * D, n, h * D:(h + 1) * D], w).then_inc(weights_in, 16)
            e.dma_start(w2cat[0:D, 0:D], w2).then_inc(weights_in, 16)
            e.dma_start(w2cat[D:D + 1, 0:D], b2.rearrange("(a n) -> a n", a=1)).then_inc(weights_in, 16)
            e.dma_start(w2t[:, D:D + 1], b2.rearrange("(n a) -> n a", a=1)).then_inc(weights_in, 16)
            e.dma_start(wg_sb[:], wg).then_inc(weights_in, 16)
            e.dma_start(bg_sb[D:D + 1, :], bg.rearrange("(a n) -> a n", a=1)).then_inc(weights_in, 16)
            e.dma_start(b1col[:], b1.rearrange("(n a) -> n a", a=1)).then_inc(weights_in, 16)
            for n, b in enumerate((b0, b2l)):
                e.dma_start(bias[:, n, :], b.rearrange("(a n) -> a n", a=1).to_broadcast([P, D])).then_inc(weights_in, 16)
            e.dma_start(X[:, 0:FULL, :], x_in[0:FULL * P, :].rearrange("(t p) f -> p t f", p=P)).then_inc(x_landed, 16)
            e.dma_start(X[0:REST, FULL, :], x_in[FULL * P:NODES, :]).then_inc(x_landed, 16)

            def fill(r):
                e.dma_start(adj[bass.ds(r * P, P), :], zero).then_inc(zeroed, 16)

            with e.Fori(0, NT + 1) as r:
                fill(r)
            e.wait_ge(dve, mark["ctl"])
            fill_end = e.snap(e.value_load(ctl[0:1, 1:2], min_val=NT + 1, max_val=MTILES))
            e.wait_ge(zeroed, 16 * (NT + 1))
            with e.Fori(NT, fill_end) as r:
                fill(r)
            e.wait_ge(zeroed, 16 * (fill_end + 1))
            e.sem_inc(fill_done, 2)

            pairs = e.snap(e.value_load(ctl[0:1, 0:1], min_val=NTP // 2, max_val=MTILES // 2))
            e.wait_ge(cells_ready, 1)
            e.wait_ge(counted, 1)
            for layer in range(3):
                with e.Fori(0, pairs) as pr:
                    use = pr + layer * pairs
                    for h in range(4):
                        e.wait_ge(rows_free, 4 * use + h + 1)
                        lo, hi = CUT[h % 2] * P, CUT[h % 2 + 1] * P
                        e.dma_start(rows[:, h, 0:hi - lo], adj[bass.ds((2 * pr + h // 2) * P, P), lo:hi]
                                    ).then_inc(rows_landed[h], 16)
                if layer == 0:
                    for b in range(ICB):
                        e.wait_ge(src_turned_copied, b + 1)
                        e.dma_start(src_rows[b * P:(b + 1) * P, :], srct[:, b % 2, :]).then_inc(srows_out[b % 2], 16)

            e.wait_ge(dve, mark["b_rows"])
            e.dma_start(b_table.rearrange("(t p) f -> p t f", p=P), AGG[:]).then_inc(table_out, 16)

            for h in range(2):
                e.wait_ge(srows_out[h], 16 * ((ICB + 1 - h) // 2))
            e.wait_ge(dve, mark["a_split"])
            items_of_rows = src_rows[0:IC, :].rearrange("(i j) e -> i (j e)", j=G)

            def load_ids(i, s, first):
                if not first:
                    e.wait_ge(ot_ready, i - 3)
                e.dma_start(SROW[:, s, :], items_of_rows[bass.ds(i, 1), :].to_broadcast([P, G * P])
                            ).then_inc(srow_landed[s], 16)

            for s in range(4):
                load_ids(s, s, True)
            with e.Fori(1, ITEMS // 4) as rnd:
                for s in range(4):
                    load_ids(4 * rnd + s, s, False)

            e.wait_ge(dve, mark["final"])
            e.dma_start(out[0:FULL * P, :].rearrange("(t p) f -> p t f", p=P), X[:, 0:FULL, :]).then_inc(stored_out, 16)
            e.dma_start(out[FULL * P:NODES, :], X[0:REST, FULL, :]).then_inc(stored_out, 16)
            e.wait_ge(stored_out, 32)

        @block.scalar
        def _(e):
            e.wait_ge(weights_turned, 1)
            e.activation(wt[:], ps[:, 5, :].rearrange("p (a b) -> p a b", a=4), ACT.Copy).then_inc(weights_copied, 1)
            e.activation(w2t[:, 0:D], ps[0:D, 6, 0:D], ACT.Copy).then_inc(weights_copied, 1)

            for k, n in enumerate(turns):
                s = plan[n]
                if k == 0:
                    e.wait_ge(dve, mark["consts_dve"])
                for bank in (0, 2):
                    e.wait_ge(turned, 4 * k + bank + 1)
                    r = slice(bank * 512, bank * 512 + 512)
                    c = None if s["bit"] is None else s["bit"] - COL_BITS
                    ins = e.activation(keys[s["dst"]][:, r], turn_ps[:, r], ACT.Copy,
                                       scale=1.0 if c is None else sign[:, c:c + 1])
                ins.then_inc(turn_out, 1)

            e.wait_ge(dve, mark["deg_plus"])
            e.activation(stat[:, 0, 0:NT], stat[:, 2, 0:NT], ACT.Sqrt).then_inc(deg_root, 1)

            e.wait_ge(dve, mark["items"])
            with e.Fori(0, ITEMS // 4) as rnd:
                for s in range(4):
                    i = 4 * rnd + s
                    t = e.snap(e.value_load(tile_tab[0:1, bass.ds(i, 1)], min_val=0, max_val=NTP - 1))
                    c = e.snap(e.value_load(chunk_tab[0:1, bass.ds(i, 1)], min_val=0, max_val=CHUNKS - G))
                    e.activation(dst_items[:, bass.ds(G * i, G)], dst_i[:, bass.ds(c, G)], ACT.Copy
                                 ).then_inc(item_copied, 1)
                    e.activation(src_items[:, bass.ds(G * i, G)], src_f[:, bass.ds(c, G)], ACT.Identity,
                                 bias=t128[:, bass.ds(t, 1)]).then_inc(item_copied, 1)

            for layer in range(3):
                for g in range(EG):
                    n, w = layer * EG + g, (min(8 * g + 8, NTP) - 8 * g) * D
                    e.wait_ge(agg_turned, n + 1)
                    if n >= 2:
                        e.wait_ge(product, n - 1)
                    e.activation(aggT[:, g % 2, 0:w], ps[:, g % 2, 0:w], ACT.Copy).then_inc(aggT_copied, 1)
                e.wait_ge(dve, mark[f"var{layer}"])
                e.activation(stat[:, 2, :], stat[:, 1, :], ACT.Sqrt).then_inc(root_ready, 1)
                if layer == 0:
                    for b in range(ICB):
                        e.wait_ge(src_turned, b + 1)
                        if b >= 2:
                            e.wait_ge(srows_out[b % 2], 16 * (b // 2))
                        e.activation(srct[:, b % 2, :], ps[:, 6 + b % 2, 0:P], ACT.Copy
                                     ).then_inc(src_turned_copied, 1)

            def copy_part(i, u, first):
                t = e.snap(e.value_load(tile_tab[0:1, bass.ds(i, 1)], min_val=0, max_val=NTP - 1))
                if not first:
                    e.wait_ge(h_ps_ready, i - 1)
                e.activation(AT[:, u, :], x3[:, bass.ds(t, 1), :].rearrange("p a f -> p (a f)"), ACT.Copy
                             ).then_inc(at_ready, 1)

            def hidden(i, u, first):
                e.wait_ge(h_ps_ready, i + 1)
                if not first:
                    e.wait_ge(g_ps_ready, i - 1)
                e.activation(H[0:D, u, :], ps[0:D, u, :], ACT.Relu, bias=b1col[:, 0:1]).then_inc(h_ready, 1)

            def gate(i, u, first):
                e.wait_ge(g_ps_ready, i + 1)
                if not first:
                    e.wait_ge(gated_ready, i - 1)
                e.activation(SG[:, u, :, :], ps[:, 2 + u, :].rearrange("p (j f) -> p j f", j=G)[:, :, D:2 * D],
                             ACT.Sigmoid).then_inc(gate_ready, 1)

            e.wait_ge(dve, mark["a_split"])
            copy_part(0, 0, True)
            for i in range(4):
                hidden(i, i % 2, i < 2)
                copy_part(i + 1, (i + 1) % 2, i + 1 < 2)
                if i:
                    gate(i - 1, (i - 1) % 2, i < 3)
            with e.Fori(1, ITEMS // 4) as rnd:
                for s in range(4):
                    i = 4 * rnd + s
                    hidden(i, s % 2, False)
                    copy_part(i + 1, (s + 1) % 2, False)
                    gate(i - 1, (s + 1) % 2, False)
            gate(ITEMS - 1, (ITEMS - 1) % 2, False)
            e.wait_ge(dve, mark["var3"])
            e.activation(stat[:, 2, :], stat[:, 1, :], ACT.Sqrt).then_inc(root_ready, 1)

        @block.tensor
        def _(e):
            e.sem_inc(hot_used, 2)
            e.sem_inc(rows_free, 4)
            e.wait_ge(consts, 12)
            e.wait_ge(weights_in, 16 * 22)
            for n in range(4):
                e.transpose(ps[:, 5, n * P:(n + 1) * P], wb[:, 1 + n, :], ident[:])
            e.transpose(ps[0:D, 6, 0:D], w2cat[0:D, 0:D], ident[0:D, 0:D]).then_inc(weights_turned, 1)
            e.wait_ge(weights_copied, 2)
            e.matmul(ps[0:D + 1, 6, D:2 * D], w2t[:, :], wg_sb[:], start=True, stop=True).then_inc(gate_weights, 1)

            for n in turns:
                e.wait_ge(sorted_step, n)
                for m in range(COLS // P):
                    ins = e.transpose(turn_ps[:, m * P:(m + 1) * P], keys[plan[n]["src"]][:, m * P:(m + 1) * P],
                                      ident[:])
                    if m % 4 == 3:
                        ins.then_inc(turned, 1)

            e.wait_ge(dve, mark["edge_cols"])
            for n in range(3):
                ins = e.transpose(ps[0:1, 4, n * P:(n + 1) * P], small[:, n:n + 1], ident[:])
            ins.then_inc(edge_rows, 1)
            e.wait_ge(dve, mark["carry_row"])
            e.matmul(ps[:, 4, 0:1], srow[0:1, 6, 0:P], ones[0:1, 0:1], start=True, stop=True)
            e.matmul(ps[:, 4, 1:2], srow[0:1, 7, 0:P], ones[0:1, 0:1], start=True, stop=True).then_inc(carry_cols, 1)
            e.wait_ge(dve, mark["run_ends"])
            for n, t in enumerate((keys[last % 2], keys[1 - last % 2])):
                if n:
                    e.wait_ge(dve, mark["turn_y0"])
                for m in range(COLS // P):
                    ins = e.transpose(turn_ps[:, m * P:(m + 1) * P], t[:, m * P:(m + 1) * P], ident[:])
                    if m % 4 == 3:
                        ins.then_inc(y_turned, 1)
            e.wait_ge(dve, mark["max_run"])
            e.transpose(ps[0:1, 4, P:2 * P], small[:, 6:7], ident[:]).then_inc(longest_row, 1)

            e.wait_ge(dve, mark["count_start"])
            with e.Fori(0, CHUNKS // (2 * HB)) as it:
                for half in range(2):
                    e.wait_ge(hot_ready, 2 * it + half + 1)
                    for c in range(HB):
                        for w in range(2):
                            ins = e.matmul(ps[:, 7, w * D:w * D + NT], hot[:, half, 2 * w, c, :],
                                           hot[:, half, 2 * w + 1, c, 0:NT], start=False, stop=False,
                                           skip_group_check=True)
                    ins.then_inc(hot_used, 1)
            e.wait_ge(hot_used, 2 + CHUNKS // HB)
            e.sem_inc(counted, 1)
            e.wait_ge(dve, mark["deg"])
            e.matmul(ps[0:1, 7, P:P + NT], ones[:, 0:1], deg[:, 1, :], start=True, stop=True).then_inc(tile_counts, 1)
            e.wait_ge(dve, mark["last_items"])
            e.matmul(ps[0:NT, 7, 192:193], srow[0:1, 4, 0:NT], ones[0:1, 0:1], start=True, stop=True
                     ).then_inc(last_item_col, 1)
            e.wait_ge(dve, mark["item_cmp"])
            e.matmul(ps[0:1, 6, 0:ITEMS], ones[0:NT, 0:1], item_cmp[:], start=True, stop=True).then_inc(item_tiles, 1)

            pairs = e.snap(e.value_load(ctl[0:1, 0:1], min_val=NTP // 2, max_val=MTILES // 2))
            weights = [(wb[:, 0, :], None), (wt[:, 1, :], wt[:, 0, :]), (wt[:, 2, :], wt[:, 3, :])]
            for layer in range(3):
                e.wait_ge(dve, mark[f"split{layer}"])
                with e.Fori(0, pairs) as pr:
                    use = pr + layer * pairs
                    for h in range(4):
                        e.wait_ge(rows_landed[h], 16 * use + 16)
                        for t in range(CUT[h % 2], CUT[h % 2 + 1]):
                            c = (t - CUT[h % 2]) * P
                            for k in range(3):
                                ins = e.matmul(acc_ps[:, t, :], rows[:, h, c:c + P],
                                               x3[:, bass.ds(2 * pr + h // 2, 1), k * D:(k + 1) * D]
                                               .rearrange("p a f -> p (a f)"),
                                               start=False, stop=False, skip_group_check=True)
                        ins.then_inc(rows_free, 1)
                e.wait_ge(rows_free, 4 * (layer + 1) * pairs + 4)
                e.sem_inc(agg_ready, 1)
                e.wait_ge(dve, mark[f"agg{layer}"])
                wa, wx = weights[layer]
                for g in range(EG):
                    n, t0, t1 = layer * EG + g, 8 * g, min(8 * g + 8, NTP)
                    if g >= 2:
                        e.wait_ge(aggT_copied, n - 1)
                    for k, t in enumerate(range(t0, t1, 2)):
                        ins = e.transpose(ps[:, g % 2, k * P:(k + 1) * P],
                                          AGG[:, t:t + 2, :].rearrange("p a f -> p (a f)"), ident[:])
                    ins.then_inc(agg_turned, 1)
                    if layer:
                        for k, t in enumerate(range(t0, t1, 2)):
                            ins = e.transpose(ps[:, 2 + g % 2, k * P:(k + 1) * P],
                                              X[:, t:t + 2, :].rearrange("p a f -> p (a f)"), ident[:])
                        ins.then_inc(x_turned, 1)
                    e.wait_ge(aggT_copied, n + 1)
                    if layer:
                        e.wait_ge(dve, mark[f"xT{layer}_{g}"])
                    if g >= 2:
                        e.wait_ge(dve, mark[f"out{layer}_{g - 2}"])
                    for k in range((t1 - t0) // 2):
                        o = ps[:, 4 + g % 2, k * P:(k + 1) * P]
                        ins = e.matmul(o, aggT[:, g % 2, k * P:(k + 1) * P], wa, start=True, stop=not layer)
                        if layer:
                            ins = e.matmul(o, xT[:, k * P:(k + 1) * P], wx, start=False, stop=True)
                    ins.then_inc(product, 1)
                if layer == 0:
                    for b in range(ICB):
                        if b >= 2:
                            e.wait_ge(src_turned_copied, b - 1)
                        else:
                            e.wait_ge(item_copied, 2 * ITEMS)
                        e.transpose(ps[:, 6 + b % 2, 0:P], src_items[:, b * P:(b + 1) * P], ident[:]
                                    ).then_inc(src_turned, 1)

            e.wait_ge(dve, mark["x2"])
            for g in range(EG):
                t0, t1 = 8 * g, min(8 * g + 8, NTP)
                if g >= 2:
                    e.wait_ge(dve, mark[f"pT_{g - 2}"])
                for k, t in enumerate(range(t0, t1, 2)):
                    ins = e.transpose(ps[:, g % 2, k * P:(k + 1) * P],
                                      X[:, t:t + 2, :].rearrange("p a f -> p (a f)"), ident[:])
                ins.then_inc(pair_turned, 1)
                e.wait_ge(dve, mark[f"pT_{g}"])
                if g >= 2:
                    e.wait_ge(dve, mark[f"p_{g - 2}"])
                for k in range((t1 - t0) // 2):
                    for w in range(2):
                        ins = e.matmul(ps[:, 2 + 2 * w + g % 2, k * P:(k + 1) * P], xT[:, k * P:(k + 1) * P],
                                       wb[:, 5 + w, :], start=True, stop=True)
                ins.then_inc(pair_product, 1)

            def hidden(i, rnd, s, first):
                u = s % 2
                e.wait_ge(at_ready, i + 1)
                e.wait_ge(ot_ready, i + 1)
                e.wait_ge(b_landed[s], 16 * G * (rnd + 1))
                if not first:
                    e.wait_ge(h_ready, i - 1)
                for k in range(3):
                    e.matmul(ps[0:D, u, :], AT[:, u, k * D:(k + 1) * D], OT[:, u, :], start=(k == 0), stop=False,
                             skip_group_check=True)
                for j in range(G):
                    ins = e.matmul(ps[0:D, u, j * P:(j + 1) * P], BGT[:, s, j, :], ident[:], start=False,
                                   stop=(j == G - 1), skip_group_check=True)
                ins.then_inc(h_ps_ready, 1)

            def interact(i, u, first):
                e.wait_ge(h_ready, i + 1)
                if not first:
                    e.wait_ge(gated_ready, i - 1)
                for j in range(G):
                    ins = e.matmul(ps[:, 2 + u, j * P:(j + 1) * P], H[0:D + 1, u, j * P:(j + 1) * P], w2cat[:],
                                   start=True, stop=True)
                ins.then_inc(g_ps_ready, 1)

            def sum_edges(i, s, first):
                u = s % 2
                e.wait_ge(gated_ready, i + 1)
                e.wait_ge(os_ready, i + 1)
                if not first:
                    e.wait_ge(sum_taken, i)
                for j in range(G):
                    ins = e.matmul(ps[:, 4 + u, 0:D], OS[:, s, j, :], MG[:, u, j, :], start=(j == 0),
                                   stop=(j == G - 1))
                ins.then_inc(sum_ready, 1)

            e.wait_ge(dve, mark["a_split"])
            for i in range(4):
                hidden(i, 0, i, i < 2)
                if i >= 1:
                    interact(i - 1, (i - 1) % 2, i < 3)
                if i >= 2:
                    sum_edges(i - 2, i - 2, i < 4)
            with e.Fori(1, ITEMS // 4) as rnd:
                for s in range(4):
                    i = 4 * rnd + s
                    hidden(i, rnd, s, False)
                    interact(i - 1, (s + 1) % 2, False)
                    sum_edges(i - 2, (s + 2) % 4, False)
            interact(ITEMS - 1, (ITEMS - 1) % 2, False)
            for i in (ITEMS - 2, ITEMS - 1):
                sum_edges(i, i % 4, False)


_INS = ["x", "src", "dst", "L0_gnn_W", "L0_gnn_b", "L1_gnn_U", "L1_gnn_V", "L2_gnn_W", "L2_gnn_b",
        "L3_gnn_W1", "L3_gnn_b1", "L3_gnn_W2", "L3_gnn_b2", "L3_gnn_Wg", "L3_gnn_bg"]


def kernel(**inputs):
    import numpy as _np
    import concourse.bacc as _bacc
    from concourse import mybir as _mybir
    from concourse.bass_utils import run_bass_kernel_spmd as _run

    nc = _bacc.Bacc("TRN2", target_bir_lowering=False, num_devices=1)
    arrays, args = {}, []
    for name in _INS:
        a = _np.ascontiguousarray(inputs[name])
        arrays[f"in_{name}_dram"] = a
        args.append(nc.dram_tensor(f"in_{name}_dram", a.shape, _mybir.dt.from_np(a.dtype), kind="ExternalInput").ap())
    args.append(nc.dram_tensor("out_0_dram", (NODES, D), _mybir.dt.float32, kind="ExternalOutput").ap())
    build_gnn(nc, *args)
    r = _run(nc, [arrays], core_ids=[0])
    return r.results[0]["out_0_dram"]
```

```python
from contextlib import ExitStack

import numpy as np

import concourse.bass as bass
from concourse import mybir
from concourse.alu_op_type import AluOpType as ALU

ACT = mybir.ActivationFunctionType
F32 = mybir.dt.float32
BF16 = mybir.dt.bfloat16
I32 = mybir.dt.int32
AX_X = mybir.AxisListType.X

P = 128
NODES = 6250
EDGES = 200000
D = 64
EPS = 1e-5

NT = -(-NODES // P)
NTP = NT + NT % 2
EG = -(-NTP // 8)
FULL = NODES // P
REST = NODES - FULL * P

ID_BITS = 13
LOG = 18
COLS = (1 << LOG) // P
COL_BITS = LOG - 7
ONE_BITS = 0x40000000
KEY_MASK = (1 << (2 * ID_BITS)) - 1
SENTINEL = float(np.uint32(ONE_BITS | KEY_MASK).view(np.float32))
EP = 125
EC = EDGES // EP
assert EP * EC == EDGES and EDGES < 1 << LOG and NODES < 1 << ID_BITS

LEVELS = 3
MCOLS = NT * P
CUT = [0, -(-NT // 2), NT]
MTILES = LEVELS * NT + 1
SKIP = 1 << 30
SC = 16
CHUNKS = -(-EDGES // (P * 2 * SC)) * 2 * SC
ROUNDS = CHUNKS // SC
HB = 8

G = 4
GROUPS = -(-EDGES // (P * G))
ITEMS = GROUPS + NT - 1
ITEMS += (-ITEMS) % 4
IC = ITEMS * G
ICB = -(-IC // P)
RING = 8
HALF_RING = RING // 2
GLAG = 2
GR = -(-GROUPS // RING) * RING


def sort_plan():
    steps, cur = [], 0

    def add(kind, **how):
        nonlocal cur
        steps.append(dict(how, kind=kind, src=cur, dst=1 - cur))
        cur = 1 - cur

    def col(bit):
        return bit - COL_BITS if bit >= COL_BITS else bit

    for k in range(1, COL_BITS):
        for j in range(k - 1, -1, -1):
            add("stage", stride=j, direction=k, unflip=False)
    add("sign", bit=COL_BITS)
    for j in range(COL_BITS - 1, -1, -1):
        add("stage", stride=j, direction=None, unflip=False)
    for k in range(COL_BITS + 1, LOG + 1):
        add("turn", bit=None)
        for j in range(k - 1, 6, -1):
            add("stage", stride=col(j), direction=col(k) if k < LOG else None, unflip=(j == k - 1))
        add("turn", bit=k if k < LOG else None)
        for j in range(6, -1, -1):
            add("stage", stride=j, direction=None, unflip=False)
    return steps


def build_gnn(nc, x_in, src_in, dst_in, w0, b0, u1, v1, w2l, b2l, w1, b1, w2, b2, wg, bg, out):
    plan = sort_plan()
    turns = [n for n, s in enumerate(plan) if s["kind"] == "turn"]
    last = len(plan)

    adj = nc.dram_tensor("adjacency", [MTILES * P, MCOLS], BF16).ap()
    adj_cells = adj.rearrange("a (b o) -> (a b) o", o=1)
    b_table = nc.dram_tensor("b_table", [NTP * P, D], F32).ap()
    src_rows = nc.dram_tensor("src_rows", [ICB * P, P], BF16).ap()

    with ExitStack() as ctx:
        def sb(name, shape, dt):
            return ctx.enter_context(nc.sbuf_tensor(name, shape, dt))

        def sem(name):
            return ctx.enter_context(nc.semaphore(name))

        ident = sb("ident", [P, P], F32)
        iota_i = sb("iota_i", [P, P], I32)
        iota_f = sb("iota_f", [P, P], F32)
        iota_b = sb("iota_b", [P, P], BF16)
        part_i = sb("part_i", [P, 8], I32)
        part_f = sb("part_f", [P, 1], F32)
        sign = sb("sign", [P, 7], F32)
        ones = sb("ones", [P, 1], F32)
        t128 = sb("t128", [P, NTP], F32)
        item_i = sb("item_i", [NT, ITEMS], I32)

        wb = sb("wb", [P, 7, P], F32)
        wt = sb("wt", [P, 4, P], F32)
        w2cat = sb("w2cat", [D + 1, 2 * D], F32)
        w2t = sb("w2t", [D, D + 1], F32)
        wg_sb = sb("wg_sb", [D, D], F32)
        bg_sb = sb("bg_sb", [D + 1, D], F32)
        bias = sb("bias", [P, 2, D], F32)
        b1col = sb("b1col", [D, 1], F32)

        x3 = sb("x3", [P, LEVELS * NT + 1, 3 * D], BF16)
        region = x3[:].rearrange("p a b -> p (a b)").bitcast(F32)

        def part(n):
            return region[:, n * COLS:(n + 1) * COLS]

        keys = [part(0), part(1)]
        same, runs, sorted_y, runs_y = part(2), part(3), part(4), part(5)
        src_ld, dst_ld = part(2).bitcast(I32)[0:EP, 0:EC], part(3).bitcast(I32)[0:EP, 0:EC]

        rows = sb("rows", [P, 4, CUT[1] * P], BF16)
        rflat = rows[:].rearrange("p a b -> p (a b)")
        hot = rflat[:, 0:2 * 2 * HB * 2 * P].rearrange("p (r w c n) -> p r w c n", r=2, w=4, c=HB)

        cells = sb("cell", [P, LEVELS * CHUNKS + SC], I32)
        digits = sb("digit", [P, LEVELS * CHUNKS + SC], BF16)
        cell = cells[:, 0:LEVELS * CHUNKS].rearrange("p (a b) -> p a b", a=LEVELS)
        digit = digits[:, 0:LEVELS * CHUNKS].rearrange("p (a b) -> p a b", a=LEVELS)
        cell_r = sb("cell_r", [P, 2, SC], I32)
        digit_r = sb("digit_r", [P, 2, SC], BF16)
        dst_pad = sb("dst_pad", [P, CHUNKS + HALF_RING * G], I32)
        dst_i = dst_pad[:, 0:CHUNKS]
        src_f = sb("src_f", [P, CHUNKS], F32)
        halves = sb("halves", [P, 4, CHUNKS], BF16)

        X = sb("X", [P, NTP, D], F32)
        AGG = sb("AGG", [P, NTP, D], F32)
        T1 = sb("T1", [P, NTP, D], F32)
        zero = T1[:].rearrange("p a b -> p (a b)").bitcast(BF16)[:, 0:MCOLS]
        tmp_i = AGG[:].rearrange("p a b -> p (a b)").bitcast(I32)[:, 0:CHUNKS]
        tmp_f = AGG[:].rearrange("p a b -> p (a b)")[:, CHUNKS:2 * CHUNKS]
        aggT = sb("aggT", [P, 2, 512], F32)
        xT = sb("xT", [P, 2, 512], F32)
        zero_col = sb("zero_col", [P, 1], F32)

        small = sb("small", [P, 16], F32)
        srow = sb("srow", [1, 8, 132], F32)
        deg = sb("deg", [P, 2, NT], F32)
        scale = sb("scale", [P, 4, NTP], F32)
        stat = sb("stat", [P, 3, NTP], F32)
        ctl = sb("ctl", [1, 4], I32)
        item_cmp = sb("item_cmp", [NT, ITEMS], F32)
        tile_tab = sb("tile_tab", [1, ITEMS + 4], I32)
        chunk_tab = sb("chunk_tab", [1, ITEMS], I32)
        group_tab = sb("group_tab", [1, ITEMS + 4], I32)
        slot_tab = sb("slot_tab", [1, ITEMS + 4], I32)
        last_use = sb("last_use", [1, GR], I32)
        group_cmp = rflat.bitcast(F32)[0:NT - 1, 0:GR]
        need_tab = sb("need_tab", [1, MTILES // 2], I32)
        src_items = halves[:].rearrange("p a b -> p (a b)").bitcast(F32)[:, 0:ICB * P]

        spare = x3[:].rearrange("p a b -> p (a b)")[:, NTP * 3 * D:]
        at = 0

        def ring(count, size, dt):
            nonlocal at
            n = count * size * (2 if dt == F32 else 1)
            v = spare[:, at:at + n]
            at += n
            return (v.bitcast(F32) if dt == F32 else v).rearrange("p (s n) -> p s n", s=count)

        BGT = ring(RING, G * D, F32).rearrange("p s (j f) -> p s j f", j=G)
        BT = ring(4, G * D, F32)
        AT = ring(4, 3 * D, BF16)
        SROW = ring(4, G * P, BF16)
        OT = ring(2, G * P, BF16)
        OS = ring(4, G * P, F32).rearrange("p s (j n) -> p s j n", j=G)
        SG = ring(2, G * D, F32).rearrange("p s (j f) -> p s j f", j=G)
        MG = ring(2, G * D, F32).rearrange("p s (j f) -> p s j f", j=G)
        H = ring(2, G * P, F32)
        srct = sb("srct", [P, 2, P], BF16)
        gidx = sb("gidx", [P, RING * G], I32)

        ps = ctx.enter_context(nc.psum_tensor("ps", [P, 8, 512], F32))
        psf = ps[:].rearrange("p b n -> p (b n)")
        turn_ps = psf[:, 0:COLS]
        acc_ps = psf[:, 0:NT * D].rearrange("p (t f) -> p t f", f=D)

        edges_in = sem("edges_in")
        x_landed = sem("x_landed")
        weights_in = sem("weights_in")
        consts = sem("consts")
        passed = sem("passed")
        dve = sem("dve")
        edge_rows = sem("edge_rows")
        carry_cols = sem("carry_cols")
        y_turned = sem("y_turned")
        longest_row = sem("longest_row")
        counted = sem("counted")
        tile_counts = sem("tile_counts")
        last_item_col = sem("last_item_col")
        item_tiles = sem("item_tiles")
        deg_root = sem("deg_root")
        weights_turned = sem("weights_turned")
        agg_turned = sem("agg_turned")
        x_turned = sem("x_turned")
        aggT_copied = sem("aggT_copied")
        xT_copied = sem("xT_copied")
        acc_zeroed = sem("acc_zeroed")
        product = sem("product")
        root_ready = sem("root_ready")
        pair_turned = sem("pair_turned")
        pair_product = sem("pair_product")
        fill_done = sem("fill_done")
        weights_copied = sem("weights_copied")
        gate_weights = sem("gate_weights")
        gidx_ready = sem("gidx_ready")
        src_turned = sem("src_turned")
        src_turned_copied = sem("src_turned_copied")
        sorted_step = sem("sorted_step")
        turned = sem("turned")
        turn_out = sem("turn_out")
        zeroed = sem("zeroed")
        cells_kept = sem("cells_kept")
        stored = [sem("stored0"), sem("stored1")]
        hot_ready = sem("hot_ready")
        hot_used = sem("hot_used")
        item_copied = sem("item_copied")
        rows_landed = [sem(f"rows_landed{n}") for n in range(4)]
        rows_free = sem("rows_free")
        pairs_split = sem("pairs_split")
        agg_ready = sem("agg_ready")
        table_out = sem("table_out")
        srows_out = [sem("srows_out0"), sem("srows_out1")]
        srow_landed = [sem(f"srow_landed{n}") for n in range(4)]
        b_landed = [sem(f"b_landed{n}") for n in range(RING)]
        groups_landed = sem("groups_landed")
        rounds_landed = sem("rounds_landed")
        group_uses = sem("group_uses")
        at_ready = sem("at_ready")
        b_copied = sem("b_copied")
        ot_ready = sem("ot_ready")
        os_ready = sem("os_ready")
        h_ps_ready = sem("h_ps_ready")
        h_ready = sem("h_ready")
        g_ps_ready = sem("g_ps_ready")
        gate_ready = sem("gate_ready")
        gated_ready = sem("gated_ready")
        sum_ready = sem("sum_ready")
        sum_taken = sem("sum_taken")
        stored_out = sem("stored_out")

        mark = {}

        class Seq:

            def __init__(self, eng, s):
                self.eng, self.s, self.n = eng, s, 0

            def done(self, ins):
                self.n += 1
                ins.then_inc(self.s, 1)
                return self.n

            def link(self, ins):
                self.done(ins)
                self.eng.wait_ge(self.s, self.n)

            def mark(self, name, ins):
                mark[name] = self.done(ins)

        block = ctx.enter_context(nc.Block())

        def repeat(col, n):
            return col.to_broadcast([col.shape[0], n])

        def over_f(v):
            return v.unsqueeze(2).to_broadcast([P, v.shape[1], D])

        @block.vector
        def _(e):
            q = Seq(e, dve)
            e.wait_ge(consts, 18)
            for b in range(7):
                ins = e.tensor_scalar(part_i[:, b:b + 1], part_i[:, b:b + 1], b, 1,
                                      ALU.logical_shift_right, ALU.bitwise_and)
            q.link(ins)
            q.link(e.tensor_copy(sign[:], part_i[:, 0:7]))
            q.link(e.tensor_scalar(sign[:], sign[:], -2.0, 1.0, ALU.mult, ALU.add))
            q.done(e.tensor_copy(iota_f[:], iota_i[:]))
            q.done(e.tensor_copy(iota_b[:], iota_i[:]))
            q.done(e.tensor_copy(part_f[:], part_i[:, 7:8]))
            q.done(e.tensor_scalar(t128[:], iota_i[:, 0:NTP], -float(P), None, ALU.mult))
            mark["consts_dve"] = q.n

            e.wait_ge(edges_in, 32)
            q.link(e.tensor_scalar(src_ld, src_ld, ID_BITS, ONE_BITS, ALU.logical_shift_left, ALU.bitwise_or))
            k_i = keys[0].bitcast(I32)
            q.link(e.tensor_tensor(k_i[0:EP, 0:EC], src_ld, dst_ld, ALU.bitwise_or))

            e.wait_ge(gate_weights, 1)
            q.done(e.tensor_tensor(w2cat[:, D:2 * D], ps[0:D + 1, 6, D:2 * D], bg_sb[:], ALU.add))

            n_turn = 0
            for n, s in enumerate(plan):
                if n:
                    e.wait_ge(sorted_step, n)
                if n and plan[n - 1]["kind"] == "turn":
                    e.wait_ge(turn_out, n_turn)
                a, b = keys[s["src"]], keys[s["dst"]]
                if s["kind"] == "sign":
                    c = s["bit"] - COL_BITS
                    ins = e.tensor_scalar(b, a, sign[:, c:c + 1], None, ALU.mult)
                elif s["kind"] == "turn":
                    for bank in (1, 3):
                        e.wait_ge(turned, 4 * n_turn + bank + 1)
                        r = slice(bank * 512, bank * 512 + 512)
                        if s["bit"] is None:
                            ins = e.tensor_copy(b[:, r], turn_ps[:, r])
                        else:
                            c = s["bit"] - COL_BITS
                            ins = e.tensor_scalar(b[:, r], turn_ps[:, r], sign[:, c:c + 1], None, ALU.mult)
                    n_turn += 1
                else:
                    cj, ck = s["stride"], s["direction"]

                    def view(t, high, down):
                        if ck is None:
                            return t.rearrange("p (a t c) -> p a t c", t=2, c=1 << cj)[:, :, high, :]
                        lo, hi = min(cj, ck), max(cj, ck)
                        w = t.rearrange("p (a t b u c) -> p a t b u c", t=2, u=2, c=1 << lo,
                                        b=1 << (hi - lo - 1))
                        return w[:, :, down, :, high, :] if ck > cj else w[:, :, high, :, down, :]

                    for down in ((0,) if ck is None else (0, 1)):
                        for high in (0, 1):
                            op = ALU.min if high == down else ALU.max
                            if s["unflip"]:
                                ins = e.scalar_tensor_tensor(out=view(b, high, down), in0=view(a, 1, down),
                                                             scalar=-1.0, in1=view(a, 0, down),
                                                             op0=ALU.mult, op1=op)
                            else:
                                ins = e.tensor_tensor(view(b, high, down), view(a, 0, down),
                                                      view(a, 1, down), op)
                ins.then_inc(sorted_step, 1)
            e.wait_ge(sorted_step, last)

            S = keys[last % 2]
            q.done(e.memset(same[:, 0:1], 0.0))
            q.link(e.tensor_tensor(same[:, 1:COLS], S[:, 1:COLS], S[:, 0:COLS - 1], ALU.is_equal))
            q.link(e.tensor_tensor_scan(runs, same, repeat(ones[:], COLS), 0.0, ALU.mult, ALU.add))
            q.done(e.tensor_copy(small[:, 0:1], S[:, 0:1]))
            q.done(e.tensor_copy(small[:, 1:2], S[:, COLS - 1:COLS]))
            q.mark("edge_cols", e.tensor_copy(small[:, 2:3], runs[:, COLS - 1:COLS]))
            e.wait_ge(edge_rows, 1)
            r_first, r_last, r_run = (srow[0:1, n, 0:P] for n in range(3))
            q.link(e.tensor_copy(srow[0:1, 0:3, 0:P], ps[0:1, 4, 0:3 * P].rearrange("p (a b) -> p a b", a=3)))
            joins = srow[0:1, 3, 0:P + 1]
            q.done(e.memset(srow[0:1, 3:8, :], 0.0))
            e.wait_ge(dve, q.n)
            q.link(e.tensor_tensor(joins[:, 1:P], r_first[:, 1:P], r_last[:, 0:P - 1], ALU.is_equal))
            q.done(e.scalar_tensor_tensor(out=srow[0:1, 4, 1:P], in0=r_run[:, 0:P - 1], scalar=float(COLS),
                                          in1=joins[:, 1:P], op0=ALU.is_equal, op1=ALU.mult))
            q.done(e.tensor_tensor(srow[0:1, 5, 1:P], r_run[:, 0:P - 1], joins[:, 1:P], ALU.mult))
            q.done(e.tensor_scalar(srow[0:1, 7, 0:P], joins[:, 1:P + 1], -1.0, 1.0, ALU.mult, ALU.add))
            e.wait_ge(dve, q.n)
            q.mark("carry_row", e.tensor_tensor_scan(srow[0:1, 6, 0:P], srow[0:1, 4, 0:P], srow[0:1, 5, 0:P],
                                                     0.0, ALU.mult, ALU.add))
            e.wait_ge(carry_cols, 1)
            q.done(e.tensor_copy(small[:, 4:6], ps[:, 4, 0:2]))
            q.done(e.memset(same[:, 0:1], 1.0))
            e.wait_ge(dve, q.n)
            q.link(e.tensor_tensor_scan(runs, same, repeat(ones[:], COLS), small[:, 4:5], ALU.mult, ALU.add))
            run_end = keys[1 - last % 2]
            q.done(e.scalar_tensor_tensor(out=run_end[:, 0:COLS - 1], in0=same[:, 1:COLS], scalar=0.0,
                                          in1=runs[:, 0:COLS - 1], op0=ALU.is_equal, op1=ALU.mult))
            q.mark("run_ends", e.tensor_tensor(run_end[:, COLS - 1:COLS], runs[:, COLS - 1:COLS],
                                               small[:, 5:6], ALU.mult))

            for n, dest in enumerate((sorted_y, runs_y)):
                d = dest.rearrange("p (h m) -> p m h", m=16)
                for bank in range(4):
                    e.wait_ge(y_turned, 4 * n + bank + 1)
                    q.done(e.tensor_copy(d[:, 4 * bank:4 * bank + 4, :],
                                         ps[:, bank, :].rearrange("p (m h) -> p m h", m=4)))
                mark[f"turn_y{n}"] = q.n
            e.wait_ge(dve, q.n)
            K = tmp_i
            q.link(e.tensor_scalar(K, sorted_y.bitcast(I32)[:, 0:CHUNKS], KEY_MASK, None, ALU.bitwise_and))
            I = keys[0].bitcast(I32)[:, 0:CHUNKS]
            J = keys[1].bitcast(I32)[:, 0:CHUNKS]
            for w, (sh, m) in enumerate(((0, 127), (7, 63), (ID_BITS, 127), (ID_BITS + 7, 63))):
                t = (I, J)[w % 2]
                q.link(e.tensor_scalar(t, K, sh, m, ALU.logical_shift_right, ALU.bitwise_and))
                q.done(e.tensor_copy(halves[:, w, :], t))
            q.link(e.tensor_scalar(same.bitcast(I32)[:, 0:CHUNKS], K, ID_BITS, None, ALU.logical_shift_right))
            q.done(e.tensor_copy(src_f[:], same.bitcast(I32)[:, 0:CHUNKS]))
            q.link(e.tensor_scalar(runs.bitcast(I32)[:, 0:CHUNKS], K, (1 << ID_BITS) - 1, None, ALU.bitwise_and))
            q.done(e.tensor_scalar(dst_i[:], runs.bitcast(I32)[:, 0:CHUNKS], NTP * P - 1, None, ALU.min))
            q.link(e.scalar_tensor_tensor(out=tmp_f, in0=halves[:, 3, :], scalar=float(NT),
                                          in1=runs_y[:, 0:CHUNKS], op0=ALU.is_lt, op1=ALU.mult))
            q.done(e.tensor_reduce(small[:, 6:7], tmp_f, AX_X, ALU.max))
            mark["max_run"] = q.n
            q.done(e.tensor_copy(I, tmp_f))
            q.done(e.tensor_scalar(J, tmp_f, 0.0, float(SKIP), ALU.is_equal, ALU.mult))
            e.wait_ge(dve, q.n)
            q.link(e.tensor_scalar(K, K, P - 1, None, ALU.bitwise_and))
            q.link(e.tensor_tensor(J, K, J, ALU.bitwise_or))
            S2, S3 = same.bitcast(I32)[:, 0:CHUNKS], K
            for lev in range(LEVELS):
                q.link(e.tensor_scalar(S2, I, 8 * lev, 255, ALU.logical_shift_right, ALU.bitwise_and))
                q.link(e.tensor_copy(digit[:, lev, :], S2))
                q.link(e.tensor_scalar(S2, src_f[:], float(NT * P * lev), float(NT), ALU.add, ALU.mult))
                q.link(e.tensor_tensor(S3, S2, halves[:, 1, :], ALU.add))
                q.link(e.tensor_scalar(S3, S3, 7, None, ALU.logical_shift_left))
                q.link(e.tensor_tensor(cell[:, lev, :], S3, J, ALU.bitwise_or))
            e.wait_ge(longest_row, 1)
            q.link(e.tensor_reduce(srow[0:1, 0, 0:1], ps[0:1, 4, 128:256], AX_X, ALU.max))
            many = srow[0:1, 0, 1:2]
            q.link(e.tensor_scalar(many, srow[0:1, 0, 0:1], 255.0, None, ALU.is_gt))
            one_level = ((NT + 1) // 2, NT + 1, ROUNDS // 2)
            all_levels = (MTILES // 2, MTILES, LEVELS * ROUNDS // 2)
            for c, (few, lots) in enumerate(zip(one_level, all_levels)):
                q.done(e.tensor_scalar(ctl[0:1, c:c + 1], many, float(lots - few), float(few), ALU.mult, ALU.add))
            mark["ctl"] = q.n

            def one_hots(half, c0):
                for w in range(4):
                    width = P if w % 2 == 0 else NT
                    ids = halves[:, w, bass.ds(c0, HB)].unsqueeze(2).to_broadcast([P, HB, width])
                    row = iota_b[:, 0:width].unsqueeze(1).to_broadcast([P, HB, width])
                    ins = e.tensor_tensor(hot[:, half, w, :, 0:width], row, ids, ALU.is_equal)
                return ins

            q.done(e.memset(ps[:, 7, :], 0.0))
            e.wait_ge(dve, q.n)
            mark["count_start"] = q.n
            with e.Fori(0, CHUNKS // (2 * HB)) as it:
                for half in range(2):
                    e.wait_ge(hot_used, 2 * it + half + 1)
                    one_hots(half, (2 * it + half) * HB).then_inc(hot_ready, 1)

            e.wait_ge(counted, 1)
            q.link(e.tensor_copy(deg[:], ps[:, 7, 0:128].rearrange("p (a b) -> p a b", a=2)[:, :, 0:NT]))
            mark["deg"] = q.n
            q.done(e.memset(src_items[:, IC:], 0.0))
            q.done(e.memset(scale[:], 0.0))
            q.done(e.tensor_scalar(stat[:, 0:2, 0:NT], deg[:], 1.0, None, ALU.max))
            e.wait_ge(dve, q.n)
            q.done(e.reciprocal(scale[:, 1:3, 0:NT], stat[:, 0:2, 0:NT]))
            q.mark("deg_plus", e.tensor_scalar(stat[:, 2, 0:NT], deg[:, 0, :], 1e-16, None, ALU.add))
            e.wait_ge(tile_counts, 1)
            q.link(e.tensor_copy(srow[0:1, 1, 0:NT], ps[0:1, 7, 128:128 + NT]))
            q.link(e.tensor_tensor_scan(srow[0:1, 2, 0:NT], repeat(ones[0:1, :], NT), srow[0:1, 1, 0:NT],
                                        0.0, ALU.mult, ALU.add))
            tile_ends = tile_tab[0:1, 0:NT]
            q.link(e.tensor_copy(tile_ends, srow[0:1, 2, 0:NT]))
            whole = NT // 2
            pair_ends = tile_ends[:, 0:2 * whole].rearrange("p (a b) -> p a b", b=2)[:, :, 1]
            q.done(e.memset(need_tab[:], float(ROUNDS - 1)))
            e.wait_ge(dve, q.n)
            q.link(e.tensor_scalar(need_tab[0:1, 0:whole], pair_ends, (P * SC).bit_length() - 1, None,
                                   ALU.logical_shift_right))
            q.link(e.tensor_scalar(srow[0:1, 5, 0:1], srow[0:1, 0, 1:2], float(LEVELS * ROUNDS - 1), None, ALU.mult))
            q.link(e.tensor_scalar(need_tab[:], need_tab[:], srow[0:1, 5, 0:1], 1.0, ALU.max, ALU.add))
            q.link(e.tensor_scalar(tile_ends, tile_ends, 9, None, ALU.logical_shift_right))
            q.link(e.tensor_copy(srow[0:1, 3, 0:NT], tile_ends))
            q.mark("last_items", e.tensor_tensor(srow[0:1, 4, 0:NT], srow[0:1, 3, 0:NT], iota_f[0:1, 0:NT], ALU.add))
            e.wait_ge(last_item_col, 1)
            q.link(e.tensor_copy(small[0:NT, 8:9], ps[0:NT, 7, 192:193]))
            q.done(e.tensor_scalar(item_cmp[:], item_i[:], small[0:NT, 8:9], None, ALU.is_gt))
            q.link(e.tensor_tensor(small[0:NT, 9:10], small[0:NT, 8:9], part_f[0:NT, :], ALU.subtract))
            q.mark("item_cmp", e.tensor_scalar(group_cmp, item_i[0:NT - 1, 0:GR], small[0:NT - 1, 9:10], None,
                                               ALU.is_ge))
            e.wait_ge(item_tiles, 1)
            q.link(e.tensor_copy(tile_tab[0:1, 0:ITEMS], ps[0:1, 6, 0:ITEMS]))
            q.link(e.tensor_tensor(chunk_tab[:], item_i[0:1, :], tile_tab[0:1, 0:ITEMS], ALU.subtract))
            q.done(e.tensor_scalar(group_tab[0:1, 0:ITEMS], chunk_tab[:], 1.0, None, ALU.add))
            q.link(e.tensor_scalar(slot_tab[0:1, 0:ITEMS], chunk_tab[:], RING - 1, None, ALU.bitwise_and))
            q.done(e.tensor_scalar(chunk_tab[:], chunk_tab[:], float(G), None, ALU.mult))
            e.wait_ge(group_uses, 1)
            q.done(e.scalar_tensor_tensor(out=last_use[:], in0=ps[0:1, 5, 0:GR], scalar=1.0,
                                          in1=item_i[0:1, 0:GR], op0=ALU.add, op1=ALU.add))
            mark["items"] = q.n

            e.wait_ge(deg_root, 1)
            q.link(e.tensor_scalar(scale[:, 3, 0:NT], deg[:, 0, :], 0.0, None, ALU.is_gt))
            q.link(e.reciprocal(stat[:, 1, 0:NT], stat[:, 0, 0:NT]))
            q.link(e.tensor_tensor(scale[:, 0, 0:NT], stat[:, 1, 0:NT], scale[:, 3, 0:NT], ALU.mult))

            def split(src, t0, t1):
                v, rest = src[:, t0:t1, :], AGG[:, t0:t1, :]
                q.link(e.tensor_copy(x3[:, t0:t1, 0:D], v))
                q.link(e.tensor_tensor(rest, v, x3[:, t0:t1, 0:D], ALU.subtract))
                q.link(e.tensor_copy(x3[:, t0:t1, D:2 * D], rest))
                q.link(e.tensor_tensor(rest, rest, x3[:, t0:t1, D:2 * D], ALU.subtract))
                q.link(e.tensor_copy(x3[:, t0:t1, 2 * D:], rest))

            def group_tiles(g):
                return 8 * g, min(8 * g + 8, NTP)

            def centre(t0, t1):
                xs, mean = X[:, t0:t1, :], stat[:, 0, t0:t1]
                q.link(e.tensor_reduce(mean, xs, AX_X, ALU.add))
                q.link(e.tensor_scalar(mean, mean, -1.0 / D, None, ALU.mult))
                q.link(e.tensor_tensor(xs, xs, over_f(mean), ALU.add))
                q.link(e.tensor_tensor(T1[:, t0:t1, :], xs, xs, ALU.mult))
                q.link(e.tensor_reduce(stat[:, 1, t0:t1], T1[:, t0:t1, :], AX_X, ALU.add))

            def variance():
                return q.done(e.tensor_scalar(stat[:, 1, :], stat[:, 1, :], 1.0 / D, EPS, ALU.mult, ALU.add))

            def inverse_root(n):
                e.wait_ge(root_ready, n)
                q.link(e.reciprocal(stat[:, 0, :], stat[:, 2, :]))

            def normalise(t0, t1):
                q.link(e.tensor_tensor(X[:, t0:t1, :], X[:, t0:t1, :], over_f(stat[:, 0, t0:t1]), ALU.mult))

            e.wait_ge(x_landed, 32)
            e.wait_ge(fill_done, 1)
            for layer in range(3):
                if layer == 0:
                    q.link(e.tensor_tensor(T1[:], X[:], over_f(scale[:, 0, :]), ALU.mult))
                else:
                    inverse_root(layer)
                for g in range(EG):
                    if layer:
                        normalise(*group_tiles(g))
                    split(X if layer else T1, *group_tiles(g))
                    if g < EG - 1:
                        e.sem_inc(pairs_split, 4)
                for lev in range(1, LEVELS):
                    q.done(e.tensor_scalar(x3[:, lev * NT:(lev + 1) * NT, :], x3[:, 0:NT, :],
                                           float(256 ** lev), None, ALU.mult))
                q.link(e.memset(x3[:, LEVELS * NT, :], 0.0))
                e.sem_inc(pairs_split, MTILES // 2 - 4 * (EG - 1))
                e.wait_ge(agg_ready, layer + 1)
                q.done(e.memset(AGG[:, NT:NTP, :], 0.0))
                for g in range(EG):
                    t0, t1 = 8 * g, min(8 * g + 8, NT)
                    if layer == 1:
                        q.done(e.tensor_copy(AGG[:, t0:t1, :], acc_ps[:, t0:t1, :]))
                    else:
                        sc = scale[:, 0 if layer == 0 else 1, t0:t1]
                        q.done(e.tensor_tensor(AGG[:, t0:t1, :], acc_ps[:, t0:t1, :], over_f(sc), ALU.mult))
                    mark[f"agg{layer}_{g}"] = q.n
                for g in range(EG):
                    t0, t1 = group_tiles(g)
                    w = (t1 - t0) * D
                    n = layer * EG + g
                    e.wait_ge(product, n + 1)
                    o = ps[:, 4 + g % 2, 0:w].rearrange("p (t f) -> p t f", f=D)
                    xs = X[:, t0:t1, :]
                    if layer == 1:
                        q.done(e.scalar_tensor_tensor(out=xs, in0=o, scalar=0.0, in1=xs, op0=ALU.max, op1=ALU.add))
                    else:
                        bb = bias[:, layer // 2, :].unsqueeze(1).to_broadcast([P, t1 - t0, D])
                        q.link(e.tensor_tensor(T1[:, t0:t1, :], o, bb, ALU.add))
                        if layer == 0:
                            q.done(e.scalar_tensor_tensor(out=xs, in0=T1[:, t0:t1, :], scalar=0.0, in1=xs,
                                                          op0=ALU.max, op1=ALU.add))
                        else:
                            q.done(e.tensor_tensor(xs, T1[:, t0:t1, :], xs, ALU.add))
                    mark[f"out{layer}_{g}"] = q.n
                    e.wait_ge(dve, q.n)
                    centre(t0, t1)
                mark[f"var{layer}"] = variance()
            inverse_root(3)
            for g in range(EG):
                normalise(*group_tiles(g))
                mark[f"x2_{g}"] = q.n

            for g in range(EG):
                t0, t1 = 8 * g, min(8 * g + 8, NTP)
                w = (t1 - t0) * D
                e.wait_ge(pair_product, g + 1)
                q.done(e.tensor_copy(T1[:, t0:t1, :], ps[:, 2 + g % 2, 0:w].rearrange("p (t f) -> p t f", f=D)))
                q.mark(f"p_{g}", e.tensor_copy(AGG[:, t0:t1, :],
                                               ps[:, 4 + g % 2, 0:w].rearrange("p (t f) -> p t f", f=D)))
            e.wait_ge(dve, q.n)
            mark["b_rows"] = q.n
            e.wait_ge(table_out, 32)
            split(T1, 0, NTP)
            q.done(e.memset(AGG[:], 0.0))
            q.done(e.memset(H[D:D + 1, :, :], 1.0))
            e.wait_ge(dve, q.n)
            mark["a_split"] = q.n

            def make_hot_t(i, rnd, s, first):
                e.wait_ge(srow_landed[s], 16 * rnd + 16)
                if not first:
                    e.wait_ge(h_ps_ready, i - 1)
                e.tensor_scalar(OT[:, s % 2, :], SROW[:, s, :], part_f[:, 0:1], None,
                                ALU.is_equal).then_inc(ot_ready, 1)

            def make_hot(i, s, first):
                if not first:
                    e.wait_ge(sum_ready, i - 3)
                for j in range(G):
                    ins = e.tensor_scalar(OS[:, s, j, :], iota_f[:], src_items[:, bass.ds(G * i + j, 1)],
                                          None, ALU.is_equal)
                ins.then_inc(os_ready, 1)

            def gated(i, u, first):
                e.wait_ge(gate_ready, i + 1)
                if not first:
                    e.wait_ge(sum_ready, i - 1)
                e.tensor_tensor(MG[:, u, :, :], SG[:, u, :, :],
                                ps[:, 2 + u, :].rearrange("p (j f) -> p j f", j=G)[:, :, 0:D],
                                ALU.mult).then_inc(gated_ready, 1)

            def add_sum(i, u):
                tile_reg = e.snap(e.value_load(tile_tab[0:1, bass.ds(i, 1)], min_val=0, max_val=NTP - 1))
                e.wait_ge(sum_ready, i + 1)
                e.wait_ge(sum_taken, i + 1)
                a = AGG[:, bass.ds(tile_reg, 1), :].rearrange("p a f -> p (a f)")
                e.tensor_tensor(a, a, ps[:, 4 + u, 0:D], ALU.add).then_inc(sum_taken, 1)

            e.sem_inc(sum_taken, 1)
            for i in range(4):
                make_hot_t(i, 0, i, i < 2)
                if i >= 2:
                    gated(i - 2, i % 2, i < 4)
                if i >= 3:
                    add_sum(i - 3, (i - 3) % 2)
                make_hot(i, i, True)
            with e.Fori(1, ITEMS // 4) as r:
                for s in range(4):
                    i = 4 * r + s
                    make_hot_t(i, r, s, False)
                    gated(i - 2, s % 2, False)
                    add_sum(i - 3, (s + 1) % 2)
                    make_hot(i, s, False)
            for i in (ITEMS - 2, ITEMS - 1):
                gated(i, i % 2, False)
            for i in range(ITEMS - 3, ITEMS):
                add_sum(i, i % 2)
            e.wait_ge(sum_taken, ITEMS + 1)
            q.link(e.tensor_tensor(AGG[:], AGG[:], over_f(scale[:, 2, :]), ALU.mult))
            q.link(e.tensor_tensor(X[:], X[:], AGG[:], ALU.add))
            centre(0, NTP)
            mark["var3"] = variance()
            inverse_root(4)
            normalise(0, CUT[1])
            mark["first_rows"] = q.n
            normalise(CUT[1], NTP)
            mark["final"] = q.n

        @block.gpsimd
        def _(e):
            def const(ins):
                ins.then_inc(consts, 1)

            const(e.memset(ident[:], 0.0))
            const(e.memset(ones[:], 1.0))
            const(e.memset(zero_col[:], 0.0))
            const(e.memset(cells[:, LEVELS * CHUNKS:], 0.0))
            const(e.memset(digits[:, LEVELS * CHUNKS:], 0.0))
            const(e.memset(dst_pad[:, CHUNKS:], 0.0))
            const(e.memset(T1[:], 0.0))
            const(e.memset(X[:], 0.0))
            const(e.memset(wb[:], 0.0))
            const(e.memset(bg_sb[:], 0.0))
            const(e.memset(keys[0], SENTINEL))
            const(e.memset(tile_tab[:], 0.0))
            const(e.memset(group_tab[:], 1.0))
            const(e.memset(slot_tab[:], 0.0))
            const(e.iota(iota_i[:], pattern=[[1, P]], base=0, channel_multiplier=0))
            const(e.iota(part_i[:], pattern=[[0, 8]], base=0, channel_multiplier=1))
            const(e.iota(item_i[:], pattern=[[1, ITEMS]], base=0, channel_multiplier=0))
            e.wait_ge(consts, 17)
            const(e.affine_select(out=ident[:], in_=ident[:], compare_op=ALU.not_equal, fill=1.0, base=0,
                                  pattern=[[-1, P]], channel_multiplier=1))

            e.wait_ge(dve, mark["ctl"])
            n_pairs = e.snap(e.value_load(ctl[0:1, 2:3], min_val=ROUNDS // 2, max_val=LEVELS * ROUNDS // 2))
            e.wait_ge(fill_done, 1)

            def keep_round(r, h):
                e.tensor_copy(cell_r[:, h, :], cells[:, bass.ds(r * SC, SC)]).then_inc(cells_kept, 1)
                e.tensor_copy(digit_r[:, h, :], digits[:, bass.ds(r * SC, SC)]).then_inc(cells_kept, 1)

            def store_round(pair, h, first):
                e.wait_ge(cells_kept, 4 * pair + 2 * h + 2)
                e.sem_inc(passed, 1)
                for c in range(SC):
                    if c == SC // 2:
                        if not first:
                            e.wait_ge(stored[1 - h], 16 * SC * (pair + h))
                            e.sem_inc(rounds_landed, 1)
                        keep_round(2 * pair + h + 1, 1 - h)
                    e.indirect_dma_start(
                        out=adj_cells, out_offset=bass.IndirectOffsetOnAxis(ap=cell_r[:, h, c:c + 1], axis=0),
                        in_=digit_r[:, h, c:c + 1], in_offset=None,
                        bounds_check=MTILES * P * MCOLS - 1, oob_is_err=False).then_inc(stored[h], 16)

            keep_round(0, 0)
            for h in range(2):
                store_round(0, h, h == 0)
            with e.Fori(1, n_pairs) as pair:
                for h in range(2):
                    store_round(pair, h, False)
            for h in range(2):
                e.wait_ge(stored[h], 16 * SC * n_pairs)
            e.sem_inc(rounds_landed, 1)

            e.wait_ge(table_out, 32)

            def keep_ids(g, half):
                n = HALF_RING * G
                e.tensor_copy(gidx[:, half * n:(half + 1) * n], dst_pad[:, bass.ds(G * g, n)]).then_inc(gidx_ready, 1)

            def gather_group(rnd, s, first):
                g = RING * rnd + s
                if not first or s >= GLAG:
                    e.wait_ge(b_landed[(s - GLAG) % RING], 16 * G * (rnd + (s >= GLAG)))
                    e.sem_inc(groups_landed, 1)
                if s == GLAG - 1 and not first:
                    keep_ids(g - s + HALF_RING, 1)
                if s == HALF_RING + GLAG - 1:
                    keep_ids(g - s + RING, 0)
                if not first:
                    used = e.snap(e.value_load(last_use[0:1, bass.ds(g - RING, 1)], min_val=1, max_val=ITEMS))
                    e.wait_ge(b_copied, used)
                if s % HALF_RING == 0:
                    e.wait_ge(gidx_ready, 2 * rnd + s // HALF_RING + 1)
                e.sem_inc(passed, 1)
                for j in range(G):
                    e.indirect_dma_start(
                        out=BGT[:, s, j, :], out_offset=None, in_=b_table,
                        in_offset=bass.IndirectOffsetOnAxis(ap=gidx[:, s * G + j:s * G + j + 1], axis=0)
                    ).then_inc(b_landed[s], 16)

            for half in range(2):
                keep_ids(half * HALF_RING, half)
            for s in range(RING):
                gather_group(0, s, True)
            with e.Fori(1, GR // RING) as rnd:
                for s in range(RING):
                    gather_group(rnd, s, False)
            for s in range(RING - GLAG, RING):
                e.wait_ge(b_landed[s], 16 * G * (GR // RING))
                e.sem_inc(groups_landed, 1)

        @block.sync
        def _(e):
            e.dma_start(src_ld, src_in.rearrange("(p n) -> p n", p=EP)).then_inc(edges_in, 16)
            e.dma_start(dst_ld, dst_in.rearrange("(p n) -> p n", p=EP)).then_inc(edges_in, 16)
            e.wait_ge(consts, 17)
            diag = [w0, u1, v1, w2l[:, 0:D], w2l[:, D:2 * D], w1[0:D, :], w1[D:2 * D, :]]
            for n, w in enumerate(diag):
                for h in range(2):
                    e.dma_start(wb[h * D:(h + 1) * D, n, h * D:(h + 1) * D], w).then_inc(weights_in, 16)
            e.dma_start(w2cat[0:D, 0:D], w2).then_inc(weights_in, 16)
            e.dma_start(w2cat[D:D + 1, 0:D], b2.rearrange("(a n) -> a n", a=1)).then_inc(weights_in, 16)
            e.dma_start(w2t[:, D:D + 1], b2.rearrange("(n a) -> n a", a=1)).then_inc(weights_in, 16)
            e.dma_start(wg_sb[:], wg).then_inc(weights_in, 16)
            e.dma_start(bg_sb[D:D + 1, :], bg.rearrange("(a n) -> a n", a=1)).then_inc(weights_in, 16)
            e.dma_start(b1col[:], b1.rearrange("(n a) -> n a", a=1)).then_inc(weights_in, 16)
            for n, b in enumerate((b0, b2l)):
                e.dma_start(bias[:, n, :], b.rearrange("(a n) -> a n", a=1).to_broadcast([P, D])).then_inc(weights_in, 16)
            e.dma_start(X[:, 0:FULL, :], x_in[0:FULL * P, :].rearrange("(t p) f -> p t f", p=P)).then_inc(x_landed, 16)
            e.dma_start(X[0:REST, FULL, :], x_in[FULL * P:NODES, :]).then_inc(x_landed, 16)

            def fill(r):
                e.dma_start(adj[bass.ds(r * P, P), :], zero).then_inc(zeroed, 16)

            with e.Fori(0, NT + 1) as r:
                fill(r)
            e.wait_ge(dve, mark["ctl"])
            fill_end = e.snap(e.value_load(ctl[0:1, 1:2], min_val=NT + 1, max_val=MTILES))
            e.wait_ge(zeroed, 16 * (NT + 1))
            with e.Fori(NT, fill_end) as r:
                fill(r)
            e.wait_ge(zeroed, 16 * (fill_end + 1))
            e.sem_inc(fill_done, 2)

            pairs = e.snap(e.value_load(ctl[0:1, 0:1], min_val=NTP // 2, max_val=MTILES // 2))
            e.wait_ge(dve, mark["items"])
            e.wait_ge(counted, 1)
            for b in range(ICB):
                e.wait_ge(src_turned_copied, b + 1)
                e.dma_start(src_rows[b * P:(b + 1) * P, :], srct[:, b % 2, :]).then_inc(srows_out[b % 2], 16)
            for layer in range(3):
                with e.Fori(0, pairs) as pr:
                    use = pr + layer * pairs
                    if layer == 0:
                        need = e.snap(e.value_load(need_tab[0:1, bass.ds(pr, 1)], min_val=1, max_val=LEVELS * ROUNDS))
                        e.wait_ge(rounds_landed, need)
                        e.sem_inc(passed, 1)
                    for h in range(4):
                        e.wait_ge(rows_free, 4 * use + h + 1)
                        lo, hi = CUT[h % 2] * P, CUT[h % 2 + 1] * P
                        e.dma_start(rows[:, h, 0:hi - lo], adj[bass.ds((2 * pr + h // 2) * P, P), lo:hi]
                                    ).then_inc(rows_landed[h], 16)

            b_tiles = b_table.rearrange("(t p) f -> p t f", p=P)
            e.wait_ge(dve, mark["p_3"])
            e.dma_start(b_tiles[:, 0:32, :], AGG[:, 0:32, :]).then_inc(table_out, 16)
            e.wait_ge(dve, mark["b_rows"])
            e.dma_start(b_tiles[:, 32:NTP, :], AGG[:, 32:NTP, :]).then_inc(table_out, 16)

            for h in range(2):
                e.wait_ge(srows_out[h], 16 * ((ICB + 1 - h) // 2))
            items_of_rows = src_rows[0:IC, :].rearrange("(i j) e -> i (j e)", j=G)

            def load_ids(i, s, first):
                if not first:
                    e.wait_ge(ot_ready, i - 3)
                e.dma_start(SROW[:, s, :], items_of_rows[bass.ds(i, 1), :].to_broadcast([P, G * P])
                            ).then_inc(srow_landed[s], 16)

            for s in range(4):
                load_ids(s, s, True)
            with e.Fori(1, ITEMS // 4) as rnd:
                for s in range(4):
                    load_ids(4 * rnd + s, s, False)

            for lo, hi, ready in ((0, CUT[1], "first_rows"), (CUT[1], FULL, "final")):
                e.wait_ge(dve, mark[ready])
                e.dma_start(out[lo * P:hi * P, :].rearrange("(t p) f -> p t f", p=P), X[:, lo:hi, :]
                            ).then_inc(stored_out, 16)
            e.dma_start(out[FULL * P:NODES, :], X[0:REST, FULL, :]).then_inc(stored_out, 16)
            e.wait_ge(stored_out, 48)

        @block.scalar
        def _(e):
            e.wait_ge(weights_turned, 1)
            e.activation(wt[:], ps[:, 5, :].rearrange("p (a b) -> p a b", a=4), ACT.Copy).then_inc(weights_copied, 1)
            e.activation(w2t[:, 0:D], ps[0:D, 6, 0:D], ACT.Copy).then_inc(weights_copied, 1)

            for k, n in enumerate(turns):
                s = plan[n]
                if k == 0:
                    e.wait_ge(dve, mark["consts_dve"])
                for bank in (0, 2):
                    e.wait_ge(turned, 4 * k + bank + 1)
                    r = slice(bank * 512, bank * 512 + 512)
                    c = None if s["bit"] is None else s["bit"] - COL_BITS
                    ins = e.activation(keys[s["dst"]][:, r], turn_ps[:, r], ACT.Copy,
                                       scale=1.0 if c is None else sign[:, c:c + 1])
                ins.then_inc(turn_out, 1)

            e.wait_ge(dve, mark["deg_plus"])
            e.activation(stat[:, 0, 0:NT], stat[:, 2, 0:NT], ACT.Sqrt).then_inc(deg_root, 1)

            e.wait_ge(dve, mark["items"])
            with e.Fori(0, ITEMS // 4) as rnd:
                for s in range(4):
                    i = 4 * rnd + s
                    t = e.snap(e.value_load(tile_tab[0:1, bass.ds(i, 1)], min_val=0, max_val=NTP - 1))
                    c = e.snap(e.value_load(chunk_tab[0:1, bass.ds(i, 1)], min_val=0, max_val=CHUNKS - G))
                    e.activation(src_items[:, bass.ds(G * i, G)], src_f[:, bass.ds(c, G)], ACT.Identity,
                                 bias=t128[:, bass.ds(t, 1)]).then_inc(item_copied, 1)
            for b in range(ICB):
                e.wait_ge(src_turned, b + 1)
                if b >= 2:
                    e.wait_ge(srows_out[b % 2], 16 * (b // 2))
                e.activation(srct[:, b % 2, :], ps[:, 6 + b % 2, 0:P], ACT.Copy).then_inc(src_turned_copied, 1)

            def zero_accumulators():
                banks = psf[:, 0:EG * 512]
                e.activation(banks, repeat(zero_col[:], EG * 512), ACT.Copy).then_inc(acc_zeroed, 1)

            e.wait_ge(src_turned_copied, ICB)
            zero_accumulators()
            for layer in range(3):
                for g in range(EG):
                    n, w = layer * EG + g, (min(8 * g + 8, NTP) - 8 * g) * D
                    e.wait_ge(agg_turned, n + 1)
                    if n >= 2:
                        e.wait_ge(product, n - 1)
                    e.activation(aggT[:, g % 2, 0:w], ps[:, g % 2, 0:w], ACT.Copy).then_inc(aggT_copied, 1)
                    if layer:
                        e.wait_ge(x_turned, n - EG + 1)
                        e.activation(xT[:, g % 2, 0:w], ps[:, 2 + g % 2, 0:w], ACT.Copy).then_inc(xT_copied, 1)
                if layer < 2:
                    e.wait_ge(dve, mark[f"out{layer}_{EG - 1}"])
                    zero_accumulators()
                e.wait_ge(dve, mark[f"var{layer}"])
                e.activation(stat[:, 2, :], stat[:, 1, :], ACT.Sqrt).then_inc(root_ready, 1)

            for g in range(EG):
                w = (min(8 * g + 8, NTP) - 8 * g) * D
                e.wait_ge(pair_turned, g + 1)
                if g >= 2:
                    e.wait_ge(pair_product, g - 1)
                e.activation(xT[:, g % 2, 0:w], ps[:, g % 2, 0:w], ACT.Copy).then_inc(xT_copied, 1)

            def copy_part(i, u, first):
                t = e.snap(e.value_load(tile_tab[0:1, bass.ds(i, 1)], min_val=0, max_val=NTP - 1))
                if not first:
                    e.wait_ge(h_ps_ready, i - 3)
                e.activation(AT[:, u, :], x3[:, bass.ds(t, 1), :].rearrange("p a f -> p (a f)"), ACT.Copy
                             ).then_inc(at_ready, 1)
                g = e.snap(e.value_load(group_tab[0:1, bass.ds(i, 1)], min_val=0, max_val=GROUPS))
                slot = e.snap(e.value_load(slot_tab[0:1, bass.ds(i, 1)], min_val=0, max_val=RING - 1))
                e.wait_ge(groups_landed, g)
                e.activation(BT[:, u, :], BGT[:, bass.ds(slot, 1), :, :].rearrange("p s j f -> p (s j f)"), ACT.Copy
                             ).then_inc(b_copied, 1)

            def hidden(i, u, first):
                e.wait_ge(h_ps_ready, i + 1)
                if not first:
                    e.wait_ge(g_ps_ready, i - 1)
                e.activation(H[0:D, u, :], ps[0:D, u, :], ACT.Relu, bias=b1col[:, 0:1]).then_inc(h_ready, 1)

            def gate(i, u, first):
                e.wait_ge(g_ps_ready, i + 1)
                if not first:
                    e.wait_ge(gated_ready, i - 1)
                e.activation(SG[:, u, :, :], ps[:, 2 + u, :].rearrange("p (j f) -> p j f", j=G)[:, :, D:2 * D],
                             ACT.Sigmoid).then_inc(gate_ready, 1)

            e.wait_ge(dve, mark["a_split"])
            copy_part(0, 0, True)
            copy_part(1, 1, True)
            for i in range(4):
                hidden(i, i % 2, i < 2)
                copy_part(i + 2, (i + 2) % 4, i < 2)
                if i:
                    gate(i - 1, (i - 1) % 2, i < 3)
            with e.Fori(1, ITEMS // 4) as rnd:
                for s in range(4):
                    i = 4 * rnd + s
                    hidden(i, s % 2, False)
                    copy_part(i + 2, (s + 2) % 4, False)
                    gate(i - 1, (s + 1) % 2, False)
            gate(ITEMS - 1, (ITEMS - 1) % 2, False)
            e.wait_ge(dve, mark["var3"])
            e.activation(stat[:, 2, :], stat[:, 1, :], ACT.Sqrt).then_inc(root_ready, 1)

        @block.tensor
        def _(e):
            e.sem_inc(hot_used, 2)
            e.sem_inc(rows_free, 4)
            e.wait_ge(consts, 18)
            e.wait_ge(weights_in, 16 * 22)
            for n in range(4):
                e.transpose(ps[:, 5, n * P:(n + 1) * P], wb[:, 1 + n, :], ident[:])
            e.transpose(ps[0:D, 6, 0:D], w2cat[0:D, 0:D], ident[0:D, 0:D]).then_inc(weights_turned, 1)
            e.wait_ge(weights_copied, 2)
            e.matmul(ps[0:D + 1, 6, D:2 * D], w2t[:, :], wg_sb[:], start=True, stop=True).then_inc(gate_weights, 1)

            for n in turns:
                e.wait_ge(sorted_step, n)
                for m in range(COLS // P):
                    ins = e.transpose(turn_ps[:, m * P:(m + 1) * P], keys[plan[n]["src"]][:, m * P:(m + 1) * P],
                                      ident[:])
                    if m % 4 == 3:
                        ins.then_inc(turned, 1)

            e.wait_ge(dve, mark["edge_cols"])
            for n in range(3):
                ins = e.transpose(ps[0:1, 4, n * P:(n + 1) * P], small[:, n:n + 1], ident[:])
            ins.then_inc(edge_rows, 1)
            e.wait_ge(dve, mark["carry_row"])
            e.matmul(ps[:, 4, 0:1], srow[0:1, 6, 0:P], ones[0:1, 0:1], start=True, stop=True)
            e.matmul(ps[:, 4, 1:2], srow[0:1, 7, 0:P], ones[0:1, 0:1], start=True, stop=True).then_inc(carry_cols, 1)
            e.wait_ge(dve, mark["run_ends"])
            for n, t in enumerate((keys[last % 2], keys[1 - last % 2])):
                if n:
                    e.wait_ge(dve, mark["turn_y0"])
                for m in range(COLS // P):
                    ins = e.transpose(turn_ps[:, m * P:(m + 1) * P], t[:, m * P:(m + 1) * P], ident[:])
                    if m % 4 == 3:
                        ins.then_inc(y_turned, 1)
            e.wait_ge(dve, mark["max_run"])
            e.transpose(ps[0:1, 4, P:2 * P], small[:, 6:7], ident[:]).then_inc(longest_row, 1)

            e.wait_ge(dve, mark["count_start"])
            with e.Fori(0, CHUNKS // (2 * HB)) as it:
                for half in range(2):
                    e.wait_ge(hot_ready, 2 * it + half + 1)
                    for c in range(HB):
                        for w in range(2):
                            ins = e.matmul(ps[:, 7, w * D:w * D + NT], hot[:, half, 2 * w, c, :],
                                           hot[:, half, 2 * w + 1, c, 0:NT], start=False, stop=False,
                                           skip_group_check=True)
                    ins.then_inc(hot_used, 1)
            e.wait_ge(hot_used, 2 + CHUNKS // HB)
            e.sem_inc(counted, 1)
            e.wait_ge(dve, mark["deg"])
            e.matmul(ps[0:1, 7, P:P + NT], ones[:, 0:1], deg[:, 1, :], start=True, stop=True).then_inc(tile_counts, 1)
            e.wait_ge(dve, mark["last_items"])
            e.matmul(ps[0:NT, 7, 192:193], srow[0:1, 4, 0:NT], ones[0:1, 0:1], start=True, stop=True
                     ).then_inc(last_item_col, 1)
            e.wait_ge(dve, mark["item_cmp"])
            e.matmul(ps[0:1, 6, 0:ITEMS], ones[0:NT, 0:1], item_cmp[:], start=True, stop=True).then_inc(item_tiles, 1)
            e.matmul(ps[0:1, 5, 0:GR], ones[0:NT - 1, 0:1], group_cmp, start=True, stop=True).then_inc(group_uses, 1)

            e.wait_ge(item_copied, ITEMS)
            for b in range(ICB):
                if b >= 2:
                    e.wait_ge(src_turned_copied, b - 1)
                e.transpose(ps[:, 6 + b % 2, 0:P], src_items[:, b * P:(b + 1) * P], ident[:]
                            ).then_inc(src_turned, 1)

            pairs = e.snap(e.value_load(ctl[0:1, 0:1], min_val=NTP // 2, max_val=MTILES // 2))
            weights = [(wb[:, 0, :], None), (wt[:, 1, :], wt[:, 0, :]), (wt[:, 2, :], wt[:, 3, :])]
            for layer in range(3):
                e.wait_ge(acc_zeroed, layer + 1)
                with e.Fori(0, pairs) as pr:
                    use = pr + layer * pairs
                    e.wait_ge(pairs_split, pr + (layer * (MTILES // 2) + 1))
                    for h in range(4):
                        e.wait_ge(rows_landed[h], 16 * use + 16)
                        for t in range(CUT[h % 2], CUT[h % 2 + 1]):
                            c = (t - CUT[h % 2]) * P
                            for k in range(3):
                                ins = e.matmul(acc_ps[:, t, :], rows[:, h, c:c + P],
                                               x3[:, bass.ds(2 * pr + h // 2, 1), k * D:(k + 1) * D]
                                               .rearrange("p a f -> p (a f)"),
                                               start=False, stop=False, skip_group_check=True)
                        ins.then_inc(rows_free, 1)
                e.wait_ge(rows_free, 4 * (layer + 1) * pairs + 4)
                e.sem_inc(agg_ready, 1)
                wa, wx = weights[layer]

                def turn_group(g):
                    n, t0, t1 = layer * EG + g, 8 * g, min(8 * g + 8, NTP)
                    e.wait_ge(dve, mark[f"agg{layer}_{g}"])
                    if g >= 2:
                        e.wait_ge(aggT_copied, n - 1)
                    for k, t in enumerate(range(t0, t1, 2)):
                        ins = e.transpose(ps[:, g % 2, k * P:(k + 1) * P],
                                          AGG[:, t:t + 2, :].rearrange("p a f -> p (a f)"), ident[:])
                    ins.then_inc(agg_turned, 1)
                    if layer:
                        e.wait_ge(dve, mark[f"agg{layer}_{2 + g % 2}"])
                        if g >= 2:
                            e.wait_ge(xT_copied, n - EG - 1)
                        for k, t in enumerate(range(t0, t1, 2)):
                            ins = e.transpose(ps[:, 2 + g % 2, k * P:(k + 1) * P],
                                              X[:, t:t + 2, :].rearrange("p a f -> p (a f)"), ident[:])
                        ins.then_inc(x_turned, 1)

                turn_group(0)
                for g in range(EG):
                    n = layer * EG + g
                    if g < EG - 1:
                        turn_group(g + 1)
                    e.wait_ge(aggT_copied, n + 1)
                    if layer:
                        e.wait_ge(xT_copied, n - EG + 1)
                    if g >= 2:
                        e.wait_ge(dve, mark[f"out{layer}_{g - 2}"])
                    else:
                        e.wait_ge(dve, mark[f"agg{layer}_{4 + g % 2}"])
                    for k in range((min(8 * g + 8, NTP) - 8 * g) // 2):
                        o = ps[:, 4 + g % 2, k * P:(k + 1) * P]
                        ins = e.matmul(o, aggT[:, g % 2, k * P:(k + 1) * P], wa, start=True, stop=not layer)
                        if layer:
                            ins = e.matmul(o, xT[:, g % 2, k * P:(k + 1) * P], wx, start=False, stop=True)
                    ins.then_inc(product, 1)

            def turn_pairs(g):
                e.wait_ge(dve, mark[f"x2_{g}"])
                if g >= 2:
                    e.wait_ge(xT_copied, 2 * EG + g - 1)
                for k, t in enumerate(range(8 * g, min(8 * g + 8, NTP), 2)):
                    ins = e.transpose(ps[:, g % 2, k * P:(k + 1) * P],
                                      X[:, t:t + 2, :].rearrange("p a f -> p (a f)"), ident[:])
                ins.then_inc(pair_turned, 1)

            turn_pairs(0)
            for g in range(EG):
                if g < EG - 1:
                    turn_pairs(g + 1)
                e.wait_ge(xT_copied, 2 * EG + g + 1)
                if g >= 2:
                    e.wait_ge(dve, mark[f"p_{g - 2}"])
                for k in range((min(8 * g + 8, NTP) - 8 * g) // 2):
                    for w in range(2):
                        ins = e.matmul(ps[:, 2 + 2 * w + g % 2, k * P:(k + 1) * P], xT[:, g % 2, k * P:(k + 1) * P],
                                       wb[:, 5 + w, :], start=True, stop=True)
                ins.then_inc(pair_product, 1)

            def hidden(i, s, first):
                u = s % 2
                e.wait_ge(at_ready, i + 1)
                e.wait_ge(ot_ready, i + 1)
                e.wait_ge(b_copied, i + 1)
                if not first:
                    e.wait_ge(h_ready, i - 1)
                for k in range(3):
                    e.matmul(ps[0:D, u, :], AT[:, s, k * D:(k + 1) * D], OT[:, u, :], start=(k == 0), stop=False,
                             skip_group_check=True)
                for j in range(G):
                    ins = e.matmul(ps[0:D, u, j * P:(j + 1) * P], BT[:, s, j * D:(j + 1) * D], ident[:], start=False,
                                   stop=(j == G - 1), skip_group_check=True)
                ins.then_inc(h_ps_ready, 1)

            def interact(i, u, first):
                e.wait_ge(h_ready, i + 1)
                if not first:
                    e.wait_ge(gated_ready, i - 1)
                for j in range(G):
                    ins = e.matmul(ps[:, 2 + u, j * P:(j + 1) * P], H[0:D + 1, u, j * P:(j + 1) * P], w2cat[:],
                                   start=True, stop=True)
                ins.then_inc(g_ps_ready, 1)

            def sum_edges(i, s, first):
                u = s % 2
                e.wait_ge(gated_ready, i + 1)
                e.wait_ge(os_ready, i + 1)
                if not first:
                    e.wait_ge(sum_taken, i)
                for j in range(G):
                    ins = e.matmul(ps[:, 4 + u, 0:D], OS[:, s, j, :], MG[:, u, j, :], start=(j == 0),
                                   stop=(j == G - 1))
                ins.then_inc(sum_ready, 1)

            e.wait_ge(dve, mark["a_split"])
            for i in range(4):
                hidden(i, i, i < 2)
                if i >= 1:
                    interact(i - 1, (i - 1) % 2, i < 3)
                if i >= 2:
                    sum_edges(i - 2, i - 2, i < 4)
            with e.Fori(1, ITEMS // 4) as rnd:
                for s in range(4):
                    i = 4 * rnd + s
                    hidden(i, s, False)
                    interact(i - 1, (s + 1) % 2, False)
                    sum_edges(i - 2, (s + 2) % 4, False)
            interact(ITEMS - 1, (ITEMS - 1) % 2, False)
            for i in (ITEMS - 2, ITEMS - 1):
                sum_edges(i, i % 4, False)


_INS = ["x", "src", "dst", "L0_gnn_W", "L0_gnn_b", "L1_gnn_U", "L1_gnn_V", "L2_gnn_W", "L2_gnn_b",
        "L3_gnn_W1", "L3_gnn_b1", "L3_gnn_W2", "L3_gnn_b2", "L3_gnn_Wg", "L3_gnn_bg"]


def kernel(**inputs):
    import numpy as _np
    import concourse.bacc as _bacc
    from concourse import mybir as _mybir
    from concourse.bass_utils import run_bass_kernel_spmd as _run

    nc = _bacc.Bacc("TRN2", target_bir_lowering=False, num_devices=1)
    arrays, args = {}, []
    for name in _INS:
        a = _np.ascontiguousarray(inputs[name])
        arrays[f"in_{name}_dram"] = a
        args.append(nc.dram_tensor(f"in_{name}_dram", a.shape, _mybir.dt.from_np(a.dtype), kind="ExternalInput").ap())
    args.append(nc.dram_tensor("out_0_dram", (NODES, D), _mybir.dt.float32, kind="ExternalOutput").ap())
    build_gnn(nc, *args)
    r = _run(nc, [arrays], core_ids=[0])
    return r.results[0]["out_0_dram"]
```
